# Optimizing a Trainium2 kernel written in Bass

```python
import numpy as np
import jax
import jax.numpy as jnp

def _softmax(x, axis=-1):
    return jax.nn.softmax(x, axis=axis)

def _gelu(x):
    return jax.nn.gelu(x, approximate=True)

def _silu(x):
    return jax.nn.silu(x)

def _sigmoid(x):
    return jax.nn.sigmoid(x)

def _layernorm(x, axis=-1, eps=1e-05):
    m = jnp.mean(x, axis=axis, keepdims=True)
    v = jnp.var(x, axis=axis, keepdims=True)
    return (x - m) / jnp.sqrt(v + eps)

def _scatter_add(tgt, idx, src, axis=0):
    return tgt.at[idx].add(src)

def _segment_sum(src, seg, n):
    return jax.ops.segment_sum(src, seg, n)
kernel_name = 'mk_seq_postln_d1_jaxref_r8_b76b44'

def setup_inputs(seed: int=0):
    np.random.seed(seed)
    _w = jnp.asarray

    def _L0_attn_setup():
        import math
        import jax, jax.numpy as jnp
        import numpy as np
        B, T, D = (4, 256, 128)
        H = 16
        DK = D // H
        key = jax.random.key(seed)
        ks = jax.random.split(key, 9)
        s = 1.0 / math.sqrt(D)
        return {'x': jax.random.normal(ks[0], (B, T, D), dtype=jnp.float32), 'Wq': jax.random.normal(ks[1], (D, D), dtype=jnp.float32) * s, 'bq': jax.random.normal(ks[2], (D,), dtype=jnp.float32) * s, 'Wk': jax.random.normal(ks[3], (D, D), dtype=jnp.float32) * s, 'bk': jax.random.normal(ks[4], (D,), dtype=jnp.float32) * s, 'Wv': jax.random.normal(ks[5], (D, D), dtype=jnp.float32) * s, 'bv': jax.random.normal(ks[6], (D,), dtype=jnp.float32) * s, 'Wo': jax.random.normal(ks[7], (D, D), dtype=jnp.float32) * s, 'bo': jax.random.normal(ks[8], (D,), dtype=jnp.float32) * s}
    _L0_attn_in = _L0_attn_setup()

    def _L0_ffn_setup():
        import jax, jax.numpy as jnp
        import numpy as np
        B, S, D = (4, 256, 128)
        P = 9
        DM = D // 4
        EPS = 1e-05

        def _mix(x, mix_kernel):
            xp = jnp.pad(x, ((0, 0), (1, 1), (0, 0)))
            return mix_kernel[0] * xp[:, :-2] + mix_kernel[1] * xp[:, 1:-1] + mix_kernel[2] * xp[:, 2:]

        def _layernorm(h, gamma, beta):
            mu = jnp.mean(h, axis=-1, keepdims=True)
            var = jnp.var(h, axis=-1, keepdims=True)
            return (h - mu) * jax.lax.rsqrt(var + EPS) * gamma + beta
        key = jax.random.key(seed)
        ks = jax.random.split(key, 12)
        sc_in = 1.0 / np.sqrt(D)
        sc_mid = 1.0 / np.sqrt(DM)
        return {'x': jax.random.normal(ks[0], (B, S, D), dtype=jnp.float32), 'mix_kernel': jax.random.normal(ks[1], (3, D), dtype=jnp.float32) * 0.5, 'W1': jax.random.normal(ks[2], (P, D, DM), dtype=jnp.float32) * sc_in, 'b1': jnp.zeros((P, DM), dtype=jnp.float32), 'W2': jax.random.normal(ks[3], (P, DM, D), dtype=jnp.float32) * sc_mid, 'b2': jnp.zeros((P, D), dtype=jnp.float32), 'Wo1': jax.random.normal(ks[4], (D, DM), dtype=jnp.float32) * sc_in, 'bo1': jnp.zeros((DM,), dtype=jnp.float32), 'Wo2': jax.random.normal(ks[5], (DM, P), dtype=jnp.float32) * sc_mid, 'bo2': jnp.zeros((P,), dtype=jnp.float32), 'gamma': jnp.ones((D,), dtype=jnp.float32), 'beta': jnp.zeros((D,), dtype=jnp.float32)}
    _L0_ffn_in = _L0_ffn_setup()
    _d = {'L0_attn_x': _L0_attn_in['x'], 'L0_attn_Wq': _L0_attn_in['Wq'], 'L0_attn_bq': _L0_attn_in['bq'], 'L0_attn_Wk': _L0_attn_in['Wk'], 'L0_attn_bk': _L0_attn_in['bk'], 'L0_attn_Wv': _L0_attn_in['Wv'], 'L0_attn_bv': _L0_attn_in['bv'], 'L0_attn_Wo': _L0_attn_in['Wo'], 'L0_attn_bo': _L0_attn_in['bo'], 'L0_ffn_mix_kernel': _L0_ffn_in['mix_kernel'], 'L0_ffn_W1': _L0_ffn_in['W1'], 'L0_ffn_b1': _L0_ffn_in['b1'], 'L0_ffn_W2': _L0_ffn_in['W2'], 'L0_ffn_b2': _L0_ffn_in['b2'], 'L0_ffn_Wo1': _L0_ffn_in['Wo1'], 'L0_ffn_bo1': _L0_ffn_in['bo1'], 'L0_ffn_Wo2': _L0_ffn_in['Wo2'], 'L0_ffn_bo2': _L0_ffn_in['bo2'], 'L0_ffn_gamma': _L0_ffn_in['gamma'], 'L0_ffn_beta': _L0_ffn_in['beta']}
    _x0 = _d['L0_attn_x']
    _d['L0_attn_x'] = jax.random.normal(jax.random.fold_in(jax.random.key(seed), 1), (4, 512, 128), dtype=_x0.dtype)
    del _x0
    return _d

def reference(L0_attn_x, L0_attn_Wq, L0_attn_bq, L0_attn_Wk, L0_attn_bk, L0_attn_Wv, L0_attn_bv, L0_attn_Wo, L0_attn_bo, L0_ffn_mix_kernel, L0_ffn_W1, L0_ffn_b1, L0_ffn_W2, L0_ffn_b2, L0_ffn_Wo1, L0_ffn_bo1, L0_ffn_Wo2, L0_ffn_bo2, L0_ffn_gamma, L0_ffn_beta):

    def _L0_attn_ref(x, Wq, bq, Wk, bk, Wv, bv, Wo, bo):
        import math
        import jax, jax.numpy as jnp
        import numpy as np
        B, T, D = (4, 256, 128)
        H = 16
        DK = D // H
        Bx, Tx, C = x.shape
        q = (x @ Wq + bq).reshape(Bx, Tx, H, DK).transpose(0, 2, 1, 3)
        k = (x @ Wk + bk).reshape(Bx, Tx, H, DK).transpose(0, 2, 1, 3)
        v = (x @ Wv + bv).reshape(Bx, Tx, H, DK).transpose(0, 2, 1, 3)
        scores = jnp.einsum('bhqd,bhkd->bhqk', q, k) / math.sqrt(DK)
        causal = jnp.tril(jnp.ones((Tx, Tx), dtype=bool))
        scores = jnp.where(causal[None, None, :, :], scores, -jnp.inf)
        attn = jax.nn.softmax(scores, axis=-1)
        out = jnp.einsum('bhqk,bhkd->bhqd', attn, v)
        out = out.transpose(0, 2, 1, 3).reshape(Bx, Tx, C)
        return out @ Wo + bo

    def _L0_ffn_ref(x, mix_kernel, W1, b1, W2, b2, Wo1, bo1, Wo2, bo2, gamma, beta):
        import jax, jax.numpy as jnp
        import numpy as np
        B, S, D = (4, 256, 128)
        P = 9
        DM = D // 4
        EPS = 1e-05

        def _mix(x, mix_kernel):
            xp = jnp.pad(x, ((0, 0), (1, 1), (0, 0)))
            return mix_kernel[0] * xp[:, :-2] + mix_kernel[1] * xp[:, 1:-1] + mix_kernel[2] * xp[:, 2:]

        def _layernorm(h, gamma, beta):
            mu = jnp.mean(h, axis=-1, keepdims=True)
            var = jnp.var(h, axis=-1, keepdims=True)
            return (h - mu) * jax.lax.rsqrt(var + EPS) * gamma + beta
        x_mixed = _mix(x, mix_kernel)
        h = jnp.einsum('bsd,pdm->bspm', x_mixed, W1) + b1
        stacked_paths = jnp.einsum('bspm,pmd->bspd', h, W2) + b2
        scores = jnp.tanh(x_mixed @ Wo1 + bo1) @ Wo2 + bo2
        idx = jnp.argmax(scores, axis=-1)
        weights = jax.nn.one_hot(idx, P, dtype=stacked_paths.dtype)
        collapsed = jnp.einsum('bspd,bsp->bsd', stacked_paths, weights)
        return _layernorm(x + collapsed, gamma, beta)
    x = L0_attn_x
    x = _layernorm(x + _L0_attn_ref(x, L0_attn_Wq, L0_attn_bq, L0_attn_Wk, L0_attn_bk, L0_attn_Wv, L0_attn_bv, L0_attn_Wo, L0_attn_bo), axis=-1)
    x = _layernorm(x + _L0_ffn_ref(x, L0_ffn_mix_kernel, L0_ffn_W1, L0_ffn_b1, L0_ffn_W2, L0_ffn_b2, L0_ffn_Wo1, L0_ffn_bo1, L0_ffn_Wo2, L0_ffn_bo2, L0_ffn_gamma, L0_ffn_beta), axis=-1)
    return x

_drawn_inputs = setup_inputs


def setup_inputs(seed=0):
    import zlib

    import numpy as np

    out = dict(_drawn_inputs(seed))
    spreads = {'L0_ffn_b1': (0.0, 0.1),
     'L0_ffn_b2': (0.0, 0.1),
     'L0_ffn_bo1': (0.0, 0.1),
     'L0_ffn_bo2': (0.0, 0.1),
     'L0_ffn_gamma': (1.0, 0.2),
     'L0_ffn_beta': (0.0, 0.1)}
    factors = {}
    for name, (base, spread) in spreads.items():
        noise = np.random.default_rng([zlib.crc32(name.encode()), seed]).standard_normal(out[name].shape)
        drawn = base * np.exp(spread * noise) if base else spread * noise
        out[name] = jnp.asarray(drawn.astype(out[name].dtype))
    for name, factor in factors.items():
        out[name] = (out[name] * factor).astype(out[name].dtype)
    return out
```

```python
from contextlib import ExitStack

import concourse.bass as bass
from concourse import mybir

ALU = mybir.AluOpType
ACT = mybir.ActivationFunctionType
AX = mybir.AxisListType
F32 = mybir.dt.float32
BF16 = mybir.dt.bfloat16

B, T, D = 4, 512, 128
H, DK = 16, 8
NP, DM = 9, 32
EPS = 1e-5
ONES = 1.0 + 127 * 2.0 ** -16
NEG = -3.0e38
NT = T // 128
W = 64
NJ = T // W
QUADS = 2
PAIRS = H // 2 // QUADS
UNITS = B * QUADS
TERMS = 6
ROWS = TERMS * DK
SHIFT = 2 * ROWS
KST = SHIFT + 6
G3 = 3
GW = 3 * DM

SCORE_BANKS = [(j, p, n) for j, n in [(0, 4), (1, 4), (2, 2), (3, 2), (4, 1), (5, 1), (6, 1), (7, 1)]
               for p in range(0, PAIRS, n)]
STEPS = len(SCORE_BANKS)
GROUPS = [[[(0, p, 0)] for p in range(PAIRS)]]
GROUPS += [[[(j, p, 0), (NJ - j, p, T - j * W)] for p in range(PAIRS)] for j in (1, 2, 3)]
GROUPS += [[[(4, p, 0), (4, p + 1, T // 2)] for p in range(0, PAIRS, 2)]]
PROB_BANKS = [(g, n, parts) for g, group in enumerate(GROUPS) for n, parts in enumerate(group)]
NB = len(PROB_BANKS)
LAG = 9
ST_BUFS, P_BUFS = 3, 3


def prob_bank_step(u, n):
    return STEPS * (u + 1) + LAG + n * STEPS // NB


PROB_AT = {}
for _u in range(UNITS):
    for _n in range(NB):
        PROB_AT.setdefault(prob_bank_step(_u, _n), []).append((_u, _n))

PROJ_OFF = {"q": 12, "k": 14, "v": STEPS + 12}
PROJ_AT = {STEPS * (2 * b - 2) + off: (b, name) for b in range(1, B) for name, off in PROJ_OFF.items()}
POST = ["o0", "o1", "attnT", "wo", "x1T", "gate1", "h0", "gate2", "h1", "h2", "onehotT", "m0", "m1", "m2", "y"]
POST_OFF = dict(o0=0, o1=2, attnT=4, wo=6, x1T=13, gate1=17, h0=19, gate2=21, h1=23, h2=25, onehotT=27,
                m0=29, m1=31, m2=33, y=35)
POST_BASE = LAG + 2
LN3_OFF = 43


def post_step(b, off):
    return STEPS * (2 * b + 3) + POST_BASE + off


POST_AT = {post_step(b, off): (b, name) for b in range(B) for name, off in POST_OFF.items()}
MOMENTS_AT = {post_step(b, off): (b, n) for b in range(B) for n, off in enumerate((POST_OFF["wo"] + 2, POST_OFF["y"] + 2, LN3_OFF))}
LN3_AT = {post_step(b, LN3_OFF): b for b in range(B)}
ALL_STEPS = post_step(B - 1, LN3_OFF) + 3


def postln_block(nc, x, xT_in, Wq, bqk_in, Wk, Wv, bv, Wo, bo, mix, W1, b1, W2, b2, Wo1, bo1, Wo2, bo2, gamma, beta, out):
    ctx = ExitStack()
    with ctx:
        def sb(name, shape, dt=F32):
            return ctx.enter_context(nc.sbuf_tensor(name, shape, dt))

        def sem(name):
            return ctx.enter_context(nc.semaphore(name))

        wq, wk = sb("wq", [128, D]), sb("wk", [128, D])
        wv, wo = sb("wv", [128, D]), sb("wo", [128, D])
        bqk_raw, bqk = sb("bqk_raw", [128, 2]), sb("bqk", [128, 1])
        bv_all, bo_all = sb("bv_all", [128, D]), sb("bo_all", [128, D])
        gamma_all, beta_all = sb("gamma_all", [128, D]), sb("beta_all", [128, D])
        mixc = sb("mixc", [128, 3])
        w1, b1c = sb("w1", [128, NP, DM]), sb("b1c", [GW, G3])
        w2 = sb("w2", [GW + NP, G3, D])
        wg1, bg1 = sb("wg1", [128, DM]), sb("bg1", [DM, 1])
        wg2 = sb("wg2", [DM + 1, NP])
        ident, identb = sb("ident", [128, 128]), sb("identb", [128, 128], BF16)
        mask_qk, mask_kq = sb("mask_qk", [128, W], BF16), sb("mask_kq", [128, W], BF16)
        spread = sb("spread", [NP, GW * G3 + NP], BF16)
        order = sb("order", [128, NT, NP])
        minus_half = sb("minus_half", [128, NT])

        xT = sb("xT", [128, T])
        qf, kf, k_rest, q_rest = sb("qf", [128, T]), sb("kf", [128, T]), sb("k_rest", [128, T]), sb("q_rest", [128, T])
        qs, ks = sb("qs", [128, 3, T], BF16), sb("ks", [128, 3, T], BF16)
        q_plain = sb("q_plain", [128, QUADS, PAIRS, T], BF16)
        k_plain = sb("k_plain", [128, QUADS, PAIRS, T], BF16)
        q_block = sb("q_block", [128, QUADS, PAIRS * NJ, 2, W], BF16)
        k_block = sb("k_block", [128, QUADS, PAIRS * NJ, 2, W], BF16)
        v_nat = sb("v_nat", [128, NJ, QUADS * PAIRS, DK])
        v_block = sb("v_block", [128, QUADS, NJ, PAIRS, 32])
        nmax, nmax_rest = sb("nmax", [128, PAIRS * NJ]), sb("nmax_rest", [128, PAIRS * NJ])
        nmax_parts = sb("nmax_parts", [128, 3, PAIRS * NJ], BF16)
        nmaxT = sb("nmaxT", [3 * PAIRS * NJ, 128], BF16)
        probs = sb("probs", [128, P_BUFS, PAIRS, T])

        o_sb = sb("o_sb", [128, QUADS, T])
        o_rden = sb("o_rden", [128, NT, PAIRS, 2])
        attn = sb("attn", [128, NT, D])
        attnT = sb("attnT", [128, T])
        xb = sb("xb", [128, NT, D])
        res = sb("res", [128, NT, D])
        stats, mv = sb("stats", [128, NT, 6]), sb("mv", [128, NT, 2])
        rstd, nmean, varp = sb("rstd", [128, NT]), sb("nmean", [128, NT]), sb("varp", [128, NT])
        x1, x1beta = sb("x1", [128, NT, D]), sb("x1beta", [128, NT, D])
        x1T = sb("x1T", [128, T + 2])
        xmid, xmix = sb("xmid", [128, T]), sb("xmix", [128, T])
        gateT = sb("gateT", [DM + 1, T])
        best, rank = sb("best", [128, NT]), sb("rank", [128, NT, NP])
        onehot = sb("onehot", [128, NT, NP])
        onehotT = sb("onehotT", [NP, T], BF16)
        hid, hid_sel = sb("hid", [GW + NP, G3, T]), sb("hid_sel", [GW + NP, G3, T])
        ffn = sb("ffn", [128, NT, D])
        fin = sb("fin", [128, NT, D])

        def bank(name):
            return ctx.enter_context(nc.psum_tensor(name, [128, 512], F32))

        score_bank = [bank(f"score_bank{i}") for i in range(2)]
        prob_bank = [bank(f"prob_bank{i}") for i in range(ST_BUFS)]
        out_bank = bank("out_bank")
        proj_bank = bank("proj_bank")
        post_bank = proj_bank if ST_BUFS == 4 else bank("post_bank")

        q_scratch = nc.dram_tensor("q_scratch", [B, QUADS, 2, TERMS, DK, PAIRS, T], BF16).ap()
        k_scratch = nc.dram_tensor("k_scratch", [B, QUADS, 2, TERMS, DK, PAIRS, T], BF16).ap()

        s_xT, s_wqk, s_wv, s_consts = sem("xT_loaded"), sem("wqk_loaded"), sem("wv_loaded"), sem("consts_loaded")
        s_xres = sem("residual_x_loaded")
        s_pool0, s_vec0, s_zero = sem("pool_setup"), sem("vector_setup"), sem("zeroed")
        s_bqk = sem("q_bias_scaled")
        s_q_mm, s_q = sem("q_product"), sem("q_ready")
        s_k_mm, s_k = sem("k_product"), sem("k_ready")
        s_v_mm, s_v = sem("v_product"), sem("v_ready")
        s_qs, s_ks = sem("q_parts_ready"), sem("k_parts_ready")
        s_qw, s_kw = sem("q_scratch_written"), sem("k_scratch_written")
        s_vb = sem("v_block_ready")
        s_sload = [sem(f"score_operands_loaded{q}") for q in range(QUADS)]
        s_tload = [sem(f"prob_operands_loaded{q}") for q in range(QUADS)]
        s_score_mm, s_score_max = sem("score_bank_filled"), sem("score_bank_reduced")
        s_nparts, s_nT_mm, s_nT, s_shift = sem("max_parts_ready"), sem("max_transposed_product"), sem("max_rows_ready"), sem("shift_rows_loaded")
        s_prob_mm, s_exp, s_pv = sem("prob_bank_filled"), sem("probs_ready"), sem("probs_used")
        s_osb = sem("attention_out_taken")
        s_post_mm, s_post = sem("post_product_ready"), sem("post_product_taken")
        s_attn, s_xb = sem("attention_scaled"), sem("residual_biased")
        s_mv, s_x1, s_x1b, s_mixed = sem("moments_ready"), sem("x1_ready"), sem("x1_beta_ready"), sem("x_mixed")
        s_x1T, s_stats, s_rstd = sem("x1T_taken"), sem("statistics_ready"), sem("inverse_deviation_ready")
        s_onehot = sem("onehot_ready")
        s_ln2, s_fin, s_stored = sem("ffn_normalised"), sem("output_ready"), sem("output_stored")
        s_vlink, s_plink = sem("vector_chain"), sem("pool_chain")

        POST_N = len(POST)
        SETUP_IDENT, SETUP_MASKS, SETUP_ALL = 1, 4, 9 + NP
        SETUP_Q_ZERO, SETUP_SHIFT, SETUP_VECTOR = 1, 3, 6

        def post_count(b, name):
            return POST_N * b + POST.index(name) + 1

        out_v = out.rearrange("b (n p) d -> b p n d", p=128)
        x_v = x.rearrange("b (n p) d -> b p n d", p=128)
        q_rows = q_scratch.rearrange("b q s t d p n -> b q (s t d) (p n)")
        k_rows = k_scratch.rearrange("b q s t d p n -> b q (s t d) (p n)")
        q_term = q_scratch.rearrange("b q s t d p n -> b t (q s) (d p n)")
        k_term = k_scratch.rearrange("b q s t d p n -> b t (q s) (d p n)")
        Q_PART = [0, 1, 2, 0, 1, 0]
        K_PART = [0, 0, 0, 1, 1, 2]

        def block_cols(t, q, rows, p, j):
            return t[0:rows, q, p * NJ + j, :, :].rearrange("r s w -> r (s w)")

        def normalise(engine, dst, src, n):
            return engine.tensor_scalar(dst[:, n, :], src[:, n, :], nmean[:, n:n + 1], rstd[:, n:n + 1], ALU.add, ALU.mult)

        def wide(t):
            return t[:, :].unsqueeze(1).broadcast_to([128, NT, D])

        def flat(t, q):
            return t[:, q, :, :].rearrange("r p n -> r (p n)")

        block = ctx.enter_context(nc.Block())

        @block.sync
        def _(sp):
            sp.dma_start(wq[:, :], Wq).then_inc(s_wqk, 16)
            sp.dma_start(xT[:, :], xT_in[0]).then_inc(s_xT, 16)
            sp.dma_start(bqk_raw[:, :], bqk_in).then_inc(s_wqk, 16)
            sp.dma_start(wk[:, :], Wk).then_inc(s_wqk, 16)
            sp.dma_start(wv[:, :], Wv).then_inc(s_wv, 16)

            def write_scratch(b):
                sp.wait_ge(s_qs, b + 1)
                for t in range(TERMS):
                    sp.dma_start(q_term[b, t], qs[:, Q_PART[t], :]).then_inc(s_qw, 16)
                sp.wait_ge(s_ks, b + 1)
                for t in range(TERMS):
                    sp.dma_start(k_term[b, t], ks[:, K_PART[t], :]).then_inc(s_kw, 16)

            def load_score_operands(u):
                b, q = divmod(u, QUADS)
                sp.wait_ge(s_qw, 16 * TERMS * (b + 1))
                if u >= QUADS:
                    sp.wait_ge(s_score_mm, STEPS * (u - QUADS + 1))
                if u < QUADS:
                    sp.wait_ge(s_vec0, SETUP_Q_ZERO)
                for s in range(2):
                    r = slice(s * ROWS, (s + 1) * ROWS)
                    sp.dma_start(q_block[r, q, :, s, :], q_rows[b, q, r].rearrange("r (c w) -> r c w", w=W)).then_inc(s_sload[q], 16)
                sp.wait_ge(s_kw, 16 * TERMS * (b + 1))
                sp.dma_start(flat(k_plain, q)[0:SHIFT, :], k_rows[b, q]).then_inc(s_sload[q], 16)

            def load_prob_operands(u):
                b, q = divmod(u, QUADS)
                if u >= QUADS:
                    sp.wait_ge(s_prob_mm, NB * (u - QUADS + 1))
                else:
                    sp.wait_ge(s_zero, 1)
                for s in range(2):
                    r = slice(s * ROWS, (s + 1) * ROWS)
                    sp.dma_start(k_block[r, q, :, s, :], k_rows[b, q, r].rearrange("r (c w) -> r c w", w=W)).then_inc(s_tload[q], 16)
                sp.dma_start(flat(q_plain, q)[0:SHIFT, :], q_rows[b, q]).then_inc(s_tload[q], 16)

            def load_shift_rows(u):
                q = u % QUADS
                sp.wait_ge(s_nT, u + 1)
                if u >= QUADS:
                    sp.wait_ge(s_prob_mm, NB * (u - QUADS + 1))
                for s in range(2):
                    sp.dma_start(flat(q_plain, q)[SHIFT + 3 * s:SHIFT + 3 * s + 3, :],
                                 nmaxT[:, s * W:(s + 1) * W]).then_inc(s_shift, 16)

            def store(b):
                sp.wait_ge(s_fin, NT * (b + 1))
                sp.dma_start(out_v[b], fin[:, :, :]).then_inc(s_stored, 16)

            write_scratch(0)
            load_score_operands(0)
            load_prob_operands(0)
            load_score_operands(1)
            sp.wait_ge(s_v_mm, 1)
            sp.dma_start(xT[:, :], xT_in[1]).then_inc(s_xT, 16)
            for dst, src in ((bv_all[:, :], bv.partition_broadcast(128)), (wo[:, :], Wo),
                             (bo_all[:, :], bo.partition_broadcast(128)),
                             (gamma_all[:, :], gamma.partition_broadcast(128)),
                             (beta_all[:, :], beta.partition_broadcast(128)),
                             (mixc[:, :], mix),
                             (w1[:, :, :], W1),
                             (b1c[:, :], b1),
                             (w2[0:GW, :, :], W2),
                             (w2[GW:GW + NP, G3 - 1, :], b2),
                             (wg1[:, :], Wo1), (bg1[:, :], bo1.unsqueeze(1)),
                             (wg2[0:DM, :], Wo2), (wg2[DM:DM + 1, :], bo2.unsqueeze(0))):
                sp.dma_start(dst, src).then_inc(s_consts, 16)
            for step in range(ALL_STEPS):
                slot, k = divmod(step, STEPS)
                if k == 0 and slot < UNITS:
                    if slot % 2 == 0 and 2 <= slot // 2 + 1 < B:
                        sp.wait_ge(s_v_mm, slot // 2 + 1)
                        sp.dma_start(xT[:, :], xT_in[slot // 2 + 1]).then_inc(s_xT, 16)
                if k == 3 and 1 <= slot <= UNITS:
                    load_shift_rows(slot - 1)
                if k == 4 and 2 <= slot + 1 < UNITS:
                    load_score_operands(slot + 1)
                if k == LAG + 1 and 1 <= slot < UNITS:
                    load_prob_operands(slot)
                if k == 16 and slot < UNITS and slot % 2 == 0 and slot // 2 + 1 < B:
                    write_scratch(slot // 2 + 1)
                if step >= post_step(0, 0) - 2 and (step - post_step(0, 0) + 2) % (2 * STEPS) == 0:
                    b = (step - post_step(0, 0) + 2) // (2 * STEPS)
                    if b < B:
                        if b >= 1:
                            sp.wait_ge(s_post, post_count(b - 1, "wo"))
                        sp.dma_start(xb[:, :, :], x_v[b]).then_inc(s_xres, 16)
                if step - 2 in LN3_AT:
                    store(LN3_AT[step - 2])
            sp.wait_ge(s_stored, 16 * B)

        @block.gpsimd
        def _(pool):
            counts = {s_qs: 1}

            def signal(ins, semaphore):
                ins.then_inc(semaphore, 1)
                counts[semaphore] = counts.get(semaphore, 0) + 1
                pool.wait_ge(semaphore, counts[semaphore])

            def link(ins):
                signal(ins, s_plink)

            link(pool.memset(ident[:, :], 0.0))
            signal(pool.affine_select(out=ident[:, :], in_=ident[:, :], compare_op=ALU.not_equal, fill=1.0, base=0,
                               pattern=[[-1, 128]], channel_multiplier=1), s_pool0)

            def split(src, parts, ready, done, b):
                pool.wait_ge(ready, b + 1)
                if b >= 1:
                    pool.wait_ge(s_qw if done is s_qs else s_kw, 16 * TERMS * b)
                link(pool.tensor_scalar(parts[:, 0, :], src[:, :], 1.0, 1.0, ALU.mult, ALU.mult))
                link(pool.tensor_tensor(k_rest[:, :], src[:, :], parts[:, 0, :], ALU.subtract))
                link(pool.tensor_scalar(parts[:, 1, :], k_rest[:, :], 1.0, 1.0, ALU.mult, ALU.mult))
                signal(pool.tensor_tensor(parts[:, 2, :], k_rest[:, :], parts[:, 1, :], ALU.subtract), done)

            signal(pool.memset(k_block[:, :, :, :, :].rearrange("r q c s w -> r (q c s w)").bitcast(F32), 0.0), s_zero)
            split(kf, ks, s_k, s_ks, 0)
            link(pool.memset(mask_qk[0:W, :], 0.0))
            link(pool.memset(mask_kq[0:W, :], 0.0))
            link(pool.memset(spread[:, :], 1.0))
            signal(pool.affine_select(out=mask_qk[0:W, :], in_=mask_qk[0:W, :], compare_op=ALU.is_ge, fill=NEG, base=0,
                               pattern=[[-1, W]], channel_multiplier=1), s_pool0)
            signal(pool.affine_select(out=mask_kq[0:W, :], in_=mask_kq[0:W, :], compare_op=ALU.is_ge, fill=NEG, base=0,
                               pattern=[[1, W]], channel_multiplier=-1), s_pool0)
            n = GW * G3 + NP
            link(pool.affine_select(out=spread[:, :], in_=spread[:, :], compare_op=ALU.is_ge, fill=0.0, base=0,
                                    pattern=[[1, n]], channel_multiplier=-DM))
            signal(pool.affine_select(out=spread[:, :], in_=spread[:, :], compare_op=ALU.is_ge, fill=0.0, base=DM - 1,
                               pattern=[[-1, n]], channel_multiplier=DM), s_pool0)
            link(pool.memset(v_block[:, :, :, :, :].rearrange("r q j p n -> r (q j p n)"), 0.0))
            signal(pool.memset(v_block[0:W, :, :, :, 16:17], 1.0), s_pool0)
            signal(pool.memset(v_block[W:128, :, :, :, 17:18], 1.0), s_pool0)
            link(pool.memset(minus_half[:, :], -0.5))
            for p in range(NP):
                signal(pool.memset(order[:, :, p:p + 1], float(NP - p)), s_pool0)
            signal(pool.memset(x1T[:, :], 0.0), s_pool0)
            signal(pool.memset(gateT[DM:DM + 1, :], 1.0), s_pool0)
            signal(pool.memset(hid[GW:GW + NP, G3 - 1, :], 1.0), s_pool0)

            def build_v_block(u):
                b, q = divmod(u, QUADS)
                pool.wait_ge(s_v, b + 1)
                if u == 0:
                    pool.wait_ge(s_consts, 16 * 14)
                    pool.wait_ge(s_pool0, SETUP_ALL)
                if u >= QUADS:
                    pool.wait_ge(s_pv, len(GROUPS) * (u - QUADS + 1))
                for s in range(2):
                    r = slice(s * W, (s + 1) * W)
                    bias = bv_all[r, :].rearrange("r (p s d) -> r p s d", s=2, d=DK)[:, q * PAIRS:(q + 1) * PAIRS, s, :]
                    signal(pool.tensor_tensor(v_block[r, q, :, :, s * DK:(s + 1) * DK],
                                       v_nat[r, :, q * PAIRS:(q + 1) * PAIRS, :],
                                       bias.unsqueeze(1).broadcast_to([W, NJ, PAIRS, DK]), ALU.add), s_vb)

            moments = [0]

            def inverse_deviation():
                moments[0] += 1
                pool.wait_ge(s_mv, NT * moments[0])
                link(pool.tensor_scalar(varp[:, :], mv[:, :, 1], EPS, 1.0, ALU.add, ALU.mult))
                link(pool.tensor_scalar(nmean[:, :], mv[:, :, 0], -1.0, 1.0, ALU.mult, ALU.mult))
                signal(pool.tensor_tensor(rstd[:, :], varp[:, :], minus_half[:, :], ALU.pow), s_rstd)

            for step in range(ALL_STEPS):
                slot, k = divmod(step, STEPS)
                if slot < UNITS and k == LAG + 1:
                    build_v_block(slot)
                if step in PROJ_AT:
                    b, name = PROJ_AT[step]
                    if name == "q":
                        split(qf, qs, s_q, s_qs, b)
                    if name == "k":
                        split(kf, ks, s_k, s_ks, b)
                if step in POST_AT:
                    b, name = POST_AT[step]
                    if name == "o0":
                        pool.wait_ge(s_xres, 16 * (b + 1))
                        signal(pool.tensor_tensor(xb[:, :, :], xb[:, :, :], wide(bo_all), ALU.add), s_xb)
                    if name == "wo":
                        inverse_deviation()
                        if b < B - 1:
                            for n in range(NT):
                                signal(normalise(pool, x1, res, n), s_x1)
                    if name == "x1T":
                        pool.wait_ge(s_x1, NT * (b + 1))
                        signal(pool.tensor_tensor(x1beta[:, :, :], x1[:, :, :], wide(beta_all), ALU.add), s_x1b)
                    if name == "y":
                        inverse_deviation()
                        if b < B - 1:
                            for n in range(NT):
                                link(normalise(pool, ffn, ffn, n))
                            link(pool.tensor_tensor(ffn[:, :, :], ffn[:, :, :], wide(gamma_all), ALU.mult))
                            signal(pool.tensor_tensor(ffn[:, :, :], ffn[:, :, :], x1beta[:, :, :], ALU.add), s_ln2)
                if step in LN3_AT:
                    b = LN3_AT[step]
                    inverse_deviation()
                    if b < B - 1:
                        if b >= 1:
                            pool.wait_ge(s_stored, 16 * b)
                        for n in range(NT):
                            signal(normalise(pool, fin, ffn, n), s_fin)

        @block.scalar
        def _(act):
            scale = float(DK) ** -0.5
            act.wait_ge(s_wqk, 48)
            act.activation(bqk[:, 0:1], bqk_raw[:, 0:1], ACT.Copy, scale=scale).then_inc(s_bqk, 1)

            def project(b, name):
                if name == "q":
                    act.wait_ge(s_q_mm, b + 1)
                    act.wait_ge(s_bqk, 1)
                    if b >= 1:
                        act.wait_ge(s_qs, b)
                    act.activation(qf[:, :], proj_bank[:, :], ACT.Identity, bias=bqk[:, 0:1], scale=scale).then_inc(s_q, 1)
                if name == "k":
                    act.wait_ge(s_k_mm, b + 1)
                    if b >= 1:
                        act.wait_ge(s_ks, b)
                    act.activation(kf[:, :], proj_bank[:, :], ACT.Identity, bias=bqk_raw[:, 1:2]).then_inc(s_k, 1)
                if name == "v":
                    act.wait_ge(s_v_mm, b + 1)
                    if b >= 1:
                        act.wait_ge(s_vb, 2 * QUADS * b)
                    act.activation(v_nat[:, :, :, :].rearrange("r j p d -> r (j p d)"), proj_bank[:, :], ACT.Copy).then_inc(s_v, 1)

            for name in ("q", "k", "v"):
                project(0, name)
            for step in range(ALL_STEPS):
                slot, k = divmod(step, STEPS)
                for u, n in PROB_AT.get(step, ()):
                    total = NB * u + n
                    g, m, _ = PROB_BANKS[n]
                    group = len(GROUPS) * u + g
                    if group >= P_BUFS and m == 0:
                        act.wait_ge(s_pv, group - P_BUFS + 1)
                    act.wait_ge(s_prob_mm, total + 1)
                    act.activation(probs[:, group % P_BUFS, m, :], prob_bank[total % ST_BUFS][:, :], ACT.Exp).then_inc(s_exp, 1)
                if k == 3 and 1 <= slot <= UNITS:
                    u = slot - 1
                    act.wait_ge(s_nT_mm, u + 1)
                    if u >= 1:
                        act.wait_ge(s_shift, 32 * u)
                    act.activation(nmaxT[:, :], proj_bank[0:3 * PAIRS * NJ, 0:W].bitcast(BF16), ACT.Copy).then_inc(s_nT, 1)
                if k == LAG + 1 and slot >= 2 and slot - 2 < UNITS:
                    u = slot - 2
                    act.wait_ge(s_pv, len(GROUPS) * (u + 1))
                    if u >= QUADS:
                        act.wait_ge(s_post_mm, post_count(u // QUADS - 1, f"o{u % QUADS}"))
                    act.activation(o_sb[:, u % QUADS, :], out_bank[:, :], ACT.Copy).then_inc(s_osb, 1)
                if step - 1 in PROJ_AT:
                    project(*PROJ_AT[step - 1])
                if step - 1 in POST_AT:
                    b, name = POST_AT[step - 1]
                    ready = post_count(b, name)
                    if name == "attnT":
                        act.wait_ge(s_post_mm, ready)
                        act.activation(attnT[:, :], post_bank[:, :], ACT.Copy).then_inc(s_post, 1)
                    if name == "x1T":
                        act.wait_ge(s_post_mm, ready)
                        if b >= 1:
                            act.wait_ge(s_mixed, b)
                        act.wait_ge(s_consts, 16 * 14)
                        act.wait_ge(s_pool0, SETUP_ALL)
                        act.activation(xmid[:, :], post_bank[:, :], ACT.Copy, scale=mixc[:, 1:2]).then_inc(s_x1T, 1)
                        act.wait_ge(s_x1T, b + 1)
                        act.activation(x1T[:, 1:T + 1], post_bank[:, :], ACT.Copy).then_inc(s_post, 1)
                    if name == "gate1":
                        act.wait_ge(s_post_mm, ready)
                        act.activation(gateT[0:DM, :], post_bank[0:DM, :], ACT.Tanh, bias=bg1[:, 0:1]).then_inc(s_post, 1)
                    if name in ("h0", "h1", "h2"):
                        g = int(name[1])
                        act.wait_ge(s_post_mm, ready)
                        act.activation(hid[0:GW, g, :], post_bank[0:GW, :], ACT.Identity, bias=b1c[:, g:g + 1]).then_inc(s_post, 1)
                    if name == "onehotT":
                        act.wait_ge(s_post_mm, ready)
                        act.activation(onehotT[:, :], post_bank[0:NP, :], ACT.Copy).then_inc(s_post, 1)

        @block.vector
        def _(dve):
            count = [0]

            def link(ins):
                count[0] += 1
                ins.then_inc(s_vlink, 1)
                dve.wait_ge(s_vlink, count[0])

            dve.memset(q_block[:, :, :, :, :].rearrange("r q c s w -> r (q c s w)").bitcast(F32), 0.0).then_inc(s_vec0, 1)
            dve.wait_ge(s_q, 1)
            link(dve.tensor_copy(qs[:, 0, :], qf[:, :]))
            link(dve.tensor_tensor(q_rest[:, :], qf[:, :], qs[:, 0, :], ALU.subtract))
            link(dve.tensor_copy(qs[:, 1, :], q_rest[:, :]))
            dve.tensor_tensor(qs[:, 2, :], q_rest[:, :], qs[:, 1, :], ALU.subtract).then_inc(s_qs, 1)
            dve.wait_ge(s_pool0, SETUP_IDENT)
            dve.tensor_copy(identb[:, :], ident[:, :]).then_inc(s_vec0, 1)
            dve.wait_ge(s_zero, 1)
            link(dve.memset(k_block[SHIFT:SHIFT + 3, :, :, 0, :].bitcast(F32), ONES))
            link(dve.memset(k_block[SHIFT:SHIFT + 6, :, :, 1, :].bitcast(F32), ONES))
            dve.memset(k_block[SHIFT:SHIFT + 3, :, :, 1, :].bitcast(F32), 0.0).then_inc(s_vec0, 1)
            dve.wait_ge(s_vec0, SETUP_SHIFT)
            dve.wait_ge(s_pool0, SETUP_MASKS)
            dve.tensor_copy(mask_qk[W:128, :], mask_qk[0:W, :]).then_inc(s_vec0, 1)
            dve.tensor_copy(mask_kq[W:128, :], mask_kq[0:W, :]).then_inc(s_vec0, 1)
            dve.tensor_copy(spread[:, GW * G3:GW * G3 + NP], identb[0:NP, 0:NP]).then_inc(s_vec0, 1)

            def statistics(b, norm):
                if norm == 2:
                    dve.wait_ge(s_ln2, b + 1)
                else:
                    dve.wait_ge(s_post, post_count(b, ("wo", "y")[norm]))
                for n in range(NT):
                    dve.bn_stats(stats[:, n, :], (res if norm == 0 else ffn)[:, n, :]).then_inc(s_stats, 1)

            def moments(b, norm):
                if norm == 0 and b >= 1:
                    dve.wait_ge(s_fin, NT * b)
                dve.wait_ge(s_stats, NT * (3 * b + norm + 1))
                for n in range(NT):
                    dve.bn_aggr(mv[:, n, :], stats[:, n, :]).then_inc(s_mv, 1)
                if b == B - 1:
                    dve.wait_ge(s_rstd, 3 * b + norm + 1)
                    if norm == 0:
                        for n in range(NT):
                            normalise(dve, x1, res, n).then_inc(s_x1, 1)
                    if norm == 1:
                        for n in range(NT):
                            ins = normalise(dve, ffn, ffn, n)
                        link(ins)
                        link(dve.tensor_tensor(ffn[:, :, :], ffn[:, :, :], wide(gamma_all), ALU.mult))
                        dve.wait_ge(s_x1b, b + 1)
                        dve.tensor_tensor(ffn[:, :, :], ffn[:, :, :], x1beta[:, :, :], ALU.add).then_inc(s_ln2, 1)
                    if norm == 2:
                        dve.wait_ge(s_stored, 16 * b)
                        for n in range(NT):
                            normalise(dve, fin, ffn, n).then_inc(s_fin, 1)

            for step in range(ALL_STEPS):
                slot, k = divmod(step, STEPS)
                if slot < UNITS:
                    j, p, n = SCORE_BANKS[k]
                    L = (j + 1) * W
                    total = STEPS * slot + k
                    dve.wait_ge(s_score_mm, total + 1)
                    dve.tensor_reduce(nmax[:, :].rearrange("r (p j) -> r p j", j=NJ)[:, p:p + n, j],
                                      score_bank[total % 2][:, 0:n * L].rearrange("r (p l) -> r p l", l=L),
                                      AX.X, ALU.max, negate=True).then_inc(s_score_max, 1)
                    if k == STEPS - 1:
                        u = slot
                        dve.wait_ge(s_score_max, STEPS * (u + 1))
                        if u >= 1:
                            dve.wait_ge(s_nT_mm, u)
                        link(dve.tensor_copy(nmax_parts[:, 0, :], nmax[:, :]))
                        link(dve.tensor_tensor(nmax_rest[:, :], nmax[:, :], nmax_parts[:, 0, :], ALU.subtract))
                        link(dve.tensor_copy(nmax_parts[:, 1, :], nmax_rest[:, :]))
                        dve.tensor_tensor(nmax_parts[:, 2, :], nmax_rest[:, :], nmax_parts[:, 1, :], ALU.subtract).then_inc(s_nparts, 1)
                if step - 1 in POST_AT:
                    b, name = POST_AT[step - 1]
                    ready = post_count(b, name)
                    if name in ("o0", "o1"):
                        q = int(name[1])
                        dve.wait_ge(s_post_mm, ready)
                        o = post_bank[:, :].rearrange("r (n p c) -> r n p c", p=PAIRS, c=32)
                        link(dve.reciprocal(o_rden[:, :, :, :], o[:, :, :, 16:18]))
                        heads = attn[:, :, q * D // 2:(q + 1) * D // 2].rearrange("r n (p s d) -> r n p s d", s=2, d=DK)
                        for s in range(2):
                            ins = dve.tensor_tensor(heads[:, :, :, s, :], o[:, :, :, s * DK:(s + 1) * DK],
                                                    o_rden[:, :, :, s:s + 1].broadcast_to([128, NT, PAIRS, DK]), ALU.mult)
                        ins.then_inc(s_post, 1)
                    if name == "wo":
                        dve.wait_ge(s_post_mm, ready)
                        dve.wait_ge(s_xb, b + 1)
                        if b >= 1:
                            dve.wait_ge(s_x1, NT * b)
                        dve.tensor_tensor(res[:, :, :].rearrange("r n d -> r (n d)"), post_bank[:, :],
                                          xb[:, :, :].rearrange("r n d -> r (n d)"), ALU.add).then_inc(s_post, 1)
                    if name == "x1T":
                        dve.wait_ge(s_post, ready)
                        link(dve.scalar_tensor_tensor(out=xmix[:, :], in0=x1T[:, 0:T], scalar=mixc[:, 0:1], in1=xmid[:, :],
                                                      op0=ALU.mult, op1=ALU.add))
                        dve.scalar_tensor_tensor(out=xmix[:, :], in0=x1T[:, 2:T + 2], scalar=mixc[:, 2:3], in1=xmix[:, :],
                                                 op0=ALU.mult, op1=ALU.add).then_inc(s_mixed, 1)
                    if name == "gate2":
                        dve.wait_ge(s_post_mm, ready)
                        sc = post_bank[:, 0:NT * NP].rearrange("r (n p) -> r n p", p=NP)
                        link(dve.tensor_reduce(best[:, :], sc, AX.X, ALU.max))
                        dve.tensor_tensor(rank[:, :, :], sc, best[:, :].unsqueeze(2).broadcast_to([128, NT, NP]),
                                          ALU.is_equal).then_inc(s_post, 1)
                        dve.wait_ge(s_post, ready)
                        link(dve.tensor_tensor(rank[:, :, :], rank[:, :, :], order[:, :, :], ALU.mult))
                        link(dve.tensor_reduce(best[:, :], rank[:, :, :], AX.X, ALU.max))
                        dve.tensor_tensor(onehot[:, :, :], rank[:, :, :], best[:, :].unsqueeze(2).broadcast_to([128, NT, NP]),
                                          ALU.is_equal).then_inc(s_onehot, 1)
                    if name in ("m0", "m1", "m2"):
                        g = int(name[1])
                        n = GW + (NP if g == G3 - 1 else 0)
                        dve.wait_ge(s_post_mm, ready)
                        dve.tensor_tensor(hid_sel[0:n, g, :], post_bank[0:n, :], hid[0:n, g, :], ALU.mult).then_inc(s_post, 1)
                    if name == "y":
                        dve.wait_ge(s_post_mm, ready)
                        if b >= 1:
                            dve.wait_ge(s_fin, NT * b)
                        dve.tensor_tensor(ffn[:, :, :].rearrange("r n d -> r (n d)"), post_bank[:, :],
                                          x1[:, :, :].rearrange("r n d -> r (n d)"), ALU.add).then_inc(s_post, 1)
                if step in MOMENTS_AT:
                    statistics(*MOMENTS_AT[step])
                if step - 1 in MOMENTS_AT:
                    moments(*MOMENTS_AT[step - 1])

        @block.tensor
        def _(pe):
            def project(b, name):
                if name == "q":
                    pe.wait_ge(s_xT, 16 * (b + 1))
                    if b == 0:
                        pe.wait_ge(s_wqk, 48)
                    else:
                        pe.wait_ge(s_v, b)
                        if b >= 2:
                            pe.wait_ge(s_nT, 2 * b - 2)
                    pe.matmul(proj_bank[:, :], wq[:, :], xT[:, :], start=True, stop=True).then_inc(s_q_mm, 1)
                if name == "k":
                    pe.wait_ge(s_q, b + 1)
                    pe.matmul(proj_bank[:, :], wk[:, :], xT[:, :], start=True, stop=True).then_inc(s_k_mm, 1)
                if name == "v":
                    pe.wait_ge(s_k, b + 1)
                    if b == 0:
                        pe.wait_ge(s_wv, 16)
                    else:
                        pe.wait_ge(s_nT, 2 * b - 1)
                    for j in range(NJ):
                        for s in range(2):
                            mm = pe.matmul(proj_bank[s * W:(s + 1) * W, j * W:(j + 1) * W], xT[:, j * W:(j + 1) * W],
                                           wv[:, :].rearrange("c (p s d) -> c s p d", s=2, d=DK)[:, s],
                                           start=True, stop=True)
                    mm.then_inc(s_v_mm, 1)

            for name in ("q", "k", "v"):
                project(0, name)
            pe.wait_ge(s_vec0, SETUP_VECTOR)
            pending = []

            def weigh(u, g):
                group = len(GROUPS) * u + g
                q = u % QUADS
                pe.wait_ge(s_exp, NB * u + sum(len(x) for x in GROUPS[:g + 1]))
                if g == 0:
                    pe.wait_ge(s_vb, 2 * (u + 1))
                    if u >= 1:
                        pe.wait_ge(s_osb, u)
                parts = {}
                for m, bank_parts in enumerate(GROUPS[g]):
                    for j, p, col in bank_parts:
                        parts.setdefault(j, []).append((p, m, col))
                for j, items in parts.items():
                    for p, m, col in items:
                        L = T - j * W
                        mm = pe.matmul(out_bank[32 * p:32 * p + 32, j * W:T], v_block[:, q, j, p, :],
                                       probs[:, group % P_BUFS, m, col:col + L],
                                       start=(g == 0), stop=(g == len(GROUPS) - 1), skip_group_check=True)
                mm.then_inc(s_pv, 1)

            for step in range(ALL_STEPS):
                slot, k = divmod(step, STEPS)
                if slot < UNITS:
                    u, q = slot, slot % QUADS
                    total = STEPS * u + k
                    if k == 0:
                        pe.wait_ge(s_sload[q], 48 * (u // QUADS + 1))
                    if total >= 2:
                        pe.wait_ge(s_score_max, total - 1)
                    j, p0, n = SCORE_BANKS[k]
                    L = (j + 1) * W
                    dst = score_bank[total % 2]
                    for i in range(n):
                        pe.matmul(dst[:, i * L:(i + 1) * L], block_cols(q_block, q, SHIFT, p0 + i, j),
                                  k_plain[0:SHIFT, q, p0 + i, 0:L], start=True, stop=False)
                        mm = pe.matmul(dst[:, (i + 1) * L - W:(i + 1) * L], identb[:, :], mask_qk[:, :], start=False, stop=True)
                    mm.then_inc(s_score_mm, 1)
                for u, n in PROB_AT.get(step, ()):
                    q = u % QUADS
                    total = NB * u + n
                    if n == 0:
                        pe.wait_ge(s_tload[q], 48 * (u // QUADS + 1))
                        pe.wait_ge(s_shift, 32 * (u + 1))
                    if total >= ST_BUFS:
                        pe.wait_ge(s_exp, total - ST_BUFS + 1)
                    dst = prob_bank[total % ST_BUFS]
                    for j, p, col in PROB_BANKS[n][2]:
                        L = T - j * W
                        pe.matmul(dst[:, col:col + L], block_cols(k_block, q, KST, p, j),
                                  q_plain[0:KST, q, p, j * W:T], start=True, stop=False)
                        mm = pe.matmul(dst[:, col:col + W], identb[:, :], mask_kq[:, :], start=False, stop=True)
                    mm.then_inc(s_prob_mm, 1)
                    g, m, _ = PROB_BANKS[n]
                    if m == len(GROUPS[g]) - 1:
                        pending.append((u, g, total))
                    while pending and (pending[0][2] <= total - 2):
                        weigh(*pending.pop(0)[:2])
                if k == LAG and slot >= 2 and slot - 2 < UNITS:
                    while pending and pending[0][0] <= slot - 2:
                        weigh(*pending.pop(0)[:2])
                if k == 2 and 1 <= slot <= UNITS:
                    u = slot - 1
                    pe.wait_ge(s_nparts, u + 1)
                    if u % 2 == 0 and u // 2 + 1 < B:
                        pe.wait_ge(s_k, u // 2 + 2)
                    if u % 2 == 1 and (u + 1) // 2 < B:
                        pe.wait_ge(s_v, (u + 1) // 2 + 1)
                    if u >= 1:
                        pe.wait_ge(s_nT, u)
                    pe.transpose(proj_bank[0:3 * PAIRS * NJ, 0:W].bitcast(BF16), nmax_parts[:, :, :].rearrange("r t c -> r (t c)"),
                                 identb[:, :]).then_inc(s_nT_mm, 1)
                if step in PROJ_AT:
                    project(*PROJ_AT[step])
                if step in POST_AT:
                    b, name = POST_AT[step]
                    if post_count(b, name) > 1:
                        pe.wait_ge(s_post, post_count(b, name) - 1)
                    if name in ("o0", "o1"):
                        q = int(name[1])
                        pe.wait_ge(s_osb, QUADS * b + q + 1)
                        for n in range(NT):
                            mm = pe.transpose(post_bank[:, n * 128:(n + 1) * 128], o_sb[:, q, n * 128:(n + 1) * 128], ident[:, :])
                    if name == "attnT":
                        for n in range(NT):
                            mm = pe.transpose(post_bank[:, n * 128:(n + 1) * 128], attn[:, n, :], ident[:, :])
                    if name == "wo":
                        pe.wait_ge(s_consts, 16 * 14)
                        for n in range(NT):
                            mm = pe.matmul(post_bank[:, n * 128:(n + 1) * 128], attnT[:, n * 128:(n + 1) * 128], wo[:, :],
                                           start=True, stop=True)
                    if name == "x1T":
                        for n in range(NT):
                            pe.wait_ge(s_x1, NT * b + n + 1)
                            mm = pe.transpose(post_bank[:, n * 128:(n + 1) * 128], x1[:, n, :], ident[:, :])
                    if name == "gate1":
                        pe.wait_ge(s_mixed, b + 1)
                        mm = pe.matmul(post_bank[0:DM, :], wg1[:, :], xmix[:, :], start=True, stop=True)
                    if name == "gate2":
                        for n in range(NT):
                            mm = pe.matmul(post_bank[:, n * NP:(n + 1) * NP], gateT[:, n * 128:(n + 1) * 128], wg2[:, :],
                                           start=True, stop=True)
                    if name in ("h0", "h1", "h2"):
                        g = int(name[1])
                        mm = pe.matmul(post_bank[0:GW, :], w1[:, 3 * g:3 * g + 3, :].rearrange("c p m -> c (p m)"), xmix[:, :],
                                       start=True, stop=True)
                    if name == "onehotT":
                        pe.wait_ge(s_onehot, b + 1)
                        for n in range(NT):
                            mm = pe.transpose(post_bank[0:NP, n * 128:(n + 1) * 128], onehot[:, n, :], ident[:, :])
                    if name in ("m0", "m1", "m2"):
                        g = int(name[1])
                        n = GW + (NP if g == G3 - 1 else 0)
                        mm = pe.matmul(post_bank[0:n, :], spread[:, g * GW:g * GW + n], onehotT[:, :], start=True, stop=True)
                    if name == "y":
                        for n in range(NT):
                            for g in range(G3):
                                r = GW + (NP if g == G3 - 1 else 0)
                                mm = pe.matmul(post_bank[:, n * 128:(n + 1) * 128], hid_sel[0:r, g, n * 128:(n + 1) * 128],
                                               w2[0:r, g, :], start=(g == 0), stop=(g == G3 - 1))
                    mm.then_inc(s_post_mm, 1)


_INS = ["x", "xT", "Wq", "bqk", "Wk", "Wv", "bv", "Wo", "bo", "mix", "W1", "b1", "W2", "b2", "Wo1", "bo1", "Wo2", "bo2",
        "gamma", "beta"]
_OUTS = [((B, T, D), "float32")]


def kernel(**inputs):
    import numpy as _np
    import concourse.bacc as _bacc
    from concourse import mybir as _mybir
    from concourse.bass_utils import run_bass_kernel_spmd as _run

    given = {n.split("_", 2)[2]: _np.asarray(a) for n, a in inputs.items() if n.startswith("L0_attn_")}
    given |= {("g" if n in ("L0_ffn_Wo1", "L0_ffn_bo1", "L0_ffn_Wo2", "L0_ffn_bo2") else "") + n.split("_", 2)[2]: _np.asarray(a)
              for n, a in inputs.items() if n.startswith("L0_ffn_")}

    def by_quad(a):
        return a.reshape(-1, QUADS, PAIRS, 2, DK).transpose(0, 1, 3, 4, 2).reshape(-1, D)

    laid = {
        "x": given["x"], "xT": given["x"].transpose(0, 2, 1),
        "Wq": by_quad(given["Wq"]), "Wk": by_quad(given["Wk"]),
        "bqk": _np.stack([by_quad(given["bq"])[0], by_quad(given["bk"])[0]], axis=1),
        "Wv": given["Wv"], "bv": given["bv"], "Wo": given["Wo"], "bo": given["bo"],
        "mix": given["mix_kernel"].T, "W1": given["W1"].transpose(1, 0, 2),
        "b1": given["b1"].reshape(G3, GW).T, "W2": given["W2"].reshape(G3, GW, D).transpose(1, 0, 2), "b2": given["b2"],
        "Wo1": given["gWo1"], "bo1": given["gbo1"], "Wo2": given["gWo2"], "bo2": given["gbo2"],
        "gamma": given["gamma"], "beta": given["beta"],
    }
    nc = _bacc.Bacc("TRN2", target_bir_lowering=False, num_devices=1)
    arrays, args = {}, []
    for name in _INS:
        a = _np.ascontiguousarray(laid[name])
        arrays[f"in_{name}_dram"] = a
        args.append(nc.dram_tensor(f"in_{name}_dram", a.shape, _mybir.dt.from_np(a.dtype), kind="ExternalInput").ap())
    for i, (shape, dtype) in enumerate(_OUTS):
        dt = _mybir.dt.from_np(_np.dtype(dtype))
        args.append(nc.dram_tensor(f"out_{i}_dram", shape, dt, kind="ExternalOutput").ap())
    postln_block(nc, *args)
    r = _run(nc, [arrays], core_ids=[0])
    return r.results[0]["out_0_dram"]
```

```python
from contextlib import ExitStack

import concourse.bass as bass
from concourse import mybir

ALU = mybir.AluOpType
ACT = mybir.ActivationFunctionType
AX = mybir.AxisListType
F32 = mybir.dt.float32
BF16 = mybir.dt.bfloat16

B, T, D = 4, 512, 128
H, DK = 16, 8
NP, DM = 9, 32
EPS = 1e-5
ONES = 1.0 + 127 * 2.0 ** -16
NEG = -3.0e38
NT = T // 128
W = 64
NJ = T // W
QUADS = 2
PAIRS = H // 2 // QUADS
UNITS = B * QUADS
TERMS = 6
ROWS = TERMS * DK
SHIFT = 2 * ROWS
KST = SHIFT + 6
G3 = 3
GW = 3 * DM

SCORE_BANKS = [(j, p, n) for j, n in [(0, 4), (1, 4), (2, 2), (3, 2), (4, 1), (5, 1), (6, 1), (7, 1)]
               for p in range(0, PAIRS, n)]
STEPS = len(SCORE_BANKS)
GROUPS = [[[(0, p, 0)] for p in range(PAIRS)]]
GROUPS += [[[(j, p, 0), (NJ - j, p, T - j * W)] for p in range(PAIRS)] for j in (1, 2, 3)]
GROUPS += [[[(4, p, 0), (4, p + 1, T // 2)] for p in range(0, PAIRS, 2)]]
PROB_BANKS = [(g, n, parts) for g, group in enumerate(GROUPS) for n, parts in enumerate(group)]
NB = len(PROB_BANKS)
LAG = 10
MAXT_OFF = 2
SCORE_LOAD_OFF = 2
PROB_LOAD_OFF = 7
WRITE_OFF = 13
VBLOCK_OFF = 8
S_BUFS, ST_BUFS, P_BUFS = 3, 2, 3


def prob_bank_step(u, n):
    return STEPS * (u + 1) + LAG + n * STEPS // NB


PROB_AT = {}
for _u in range(UNITS):
    for _n in range(NB):
        PROB_AT.setdefault(prob_bank_step(_u, _n), []).append((_u, _n))

PROJ_OFFS = {1: {"q": 12, "k": 21, "v": 41}, 2: {"q": 11, "k": 15, "v": 34}, 3: {"q": 6, "k": 11, "v": 36}}
PROJ_AT = {STEPS * (2 * b - 2) + off: (b, name) for b in range(1, B) for name, off in PROJ_OFFS[b].items()}
POST = ["o0", "o1", "attnT", "wo", "x1T", "h0", "gate", "h1", "h2", "onehotT", "m0", "m1", "m2", "y"]
TAKEN_BY = {name: "act" if name in ("attnT", "h0", "h1", "h2", "onehotT") else "dve" for name in POST}
POST_OFF = dict(o0=2, o1=4, attnT=8, wo=10, ln1=12, x1T=19, h0=24, gate=26, h1=28, h2=35, onehotT=31, m0=39, m1=34,
                m2=41, y=44, ln2=46, ln3=60)
POST_OFF_LAST_BUT_ONE = dict(o0=2, o1=4, attnT=7, wo=11, ln1=15, x1T=22, h0=29, gate=32, h1=42, h2=34, onehotT=37,
                             m0=41, m1=50, m2=46, y=58, ln2=59, ln3=72)
POST_OFF_LAST = dict(o0=-21, o1=0, attnT=4, wo=8, ln1=13, x1T=22, h0=38, gate=71, h1=79, h2=61, onehotT=81, m0=91,
                     m1=94, m2=109, y=113, ln2=114, ln3=116)
POST_OFFS = [POST_OFF] * (B - 2) + [POST_OFF_LAST_BUT_ONE, POST_OFF_LAST]
POST_BASE = LAG + 2


def on_vector(b, norm):
    return norm >= 1 and b >= B - 2


def post_step(b, name):
    return STEPS * (2 * b + 3) + POST_BASE + POST_OFFS[b][name]


POST_AT = {}
for _b in range(B):
    for _name in POST:
        assert post_step(_b, _name) not in POST_AT
        POST_AT[post_step(_b, _name)] = _b, _name
POST_ORDER = [POST_AT[step] for step in sorted(POST_AT)]
TAKEN_ORDER = {engine: [stage for _, stage in sorted(((step + (name == "x1T"), name == "x1T"), (b, name))
                                                     for step, (b, name) in POST_AT.items() if TAKEN_BY[name] == engine)]
               for engine in ("act", "dve")}
MOMENTS_AT = {}
for _b in range(B):
    for _n, _step in enumerate((post_step(_b, "ln1"), post_step(_b, "ln2"), post_step(_b, "ln3"))):
        assert _step not in MOMENTS_AT
        MOMENTS_AT[_step] = _b, _n
MOMENTS_ORDER = [MOMENTS_AT[step] for step in sorted(MOMENTS_AT)]
STORE_AT = {post_step(b, "ln3") + 2: b for b in range(B)}
SCORES_END = STEPS * UNITS
ALL_STEPS = post_step(B - 1, "ln3") + 3


def postln_block(nc, x, xT_in, Wq, bqk_in, Wk, Wv, bv, Wo, bo, mix, W1, b1, W2, b2, Wo1, bo1, Wo2, bo2, gamma, beta, out):
    ctx = ExitStack()
    with ctx:
        def sb(name, shape, dt=F32):
            return ctx.enter_context(nc.sbuf_tensor(name, shape, dt))

        def sem(name):
            return ctx.enter_context(nc.semaphore(name))

        wq, wk = sb("wq", [128, D]), sb("wk", [128, D])
        wv, wo = sb("wv", [128, D]), sb("wo", [128, D])
        bqk_raw, bqk = sb("bqk_raw", [128, 2]), sb("bqk", [128, 1])
        bv_all, bo_all = sb("bv_all", [128, D]), sb("bo_all", [128, D])
        gamma_all, beta_all = sb("gamma_all", [128, D]), sb("beta_all", [128, D])
        mixc = sb("mixc", [128, 3])
        w1, b1c = sb("w1", [128, (NP + 1) * DM]), sb("b1c", [GW, G3])
        w2 = sb("w2", [GW + NP, G3, D])
        bg1 = sb("bg1", [128, 1])
        wg2, bg2 = sb("wg2", [128, NP]), sb("bg2", [128, NP])
        ident, identb = sb("ident", [128, 128]), sb("identb", [128, 128], BF16)
        mask_qk, mask_kq = sb("mask_qk", [128, W], BF16), sb("mask_kq", [128, W], BF16)
        spread = sb("spread", [NP, GW * G3 + NP], BF16)
        order = sb("order", [128, NT, NP])
        minus_half = sb("minus_half", [128, NT])

        xT = sb("xT", [128, 2, T])
        qf, kf, k_rest, q_rest = sb("qf", [128, T]), sb("kf", [128, T]), sb("k_rest", [128, T]), sb("q_rest", [128, T])
        qs, ks = sb("qs", [128, 3, T], BF16), sb("ks", [128, 3, T], BF16)
        q_plain = sb("q_plain", [128, QUADS, PAIRS, T], BF16)
        k_plain = sb("k_plain", [128, QUADS, PAIRS, T], BF16)
        q_block = sb("q_block", [128, QUADS, PAIRS * NJ, 2, W], BF16)
        k_block = sb("k_block", [128, QUADS, PAIRS * NJ, 2, W], BF16)
        v_nat = sb("v_nat", [128, NJ, QUADS * PAIRS, DK])
        v_block = sb("v_block", [128, QUADS, NJ, PAIRS, 32])
        nmax, nmax_rest = sb("nmax", [128, PAIRS * NJ]), sb("nmax_rest", [128, PAIRS * NJ])
        nmax_parts = sb("nmax_parts", [128, 3, PAIRS * NJ], BF16)
        nmaxT = sb("nmaxT", [3 * PAIRS * NJ, 128], BF16)
        probs = sb("probs", [128, P_BUFS, PAIRS, T])

        o_sb = sb("o_sb", [128, QUADS, T])
        class WorkBuffers:
            def __init__(w, i):
                w.o_rden = sb(f"o_rden{i}", [128, NT, PAIRS, 2])
                w.attn, w.attnT = sb(f"attn{i}", [128, NT, D]), sb(f"attnT{i}", [128, T])
                w.xb, w.res = sb(f"xb{i}", [128, NT, D]), sb(f"res{i}", [128, NT, D])
                w.stats, w.mv = sb(f"stats{i}", [128, NT, 6]), sb(f"mv{i}", [128, NT, 2])
                w.rstd, w.nmean, w.varp = sb(f"rstd{i}", [128, NT]), sb(f"nmean{i}", [128, NT]), sb(f"varp{i}", [128, NT])
                w.x1, w.x1beta = sb(f"x1{i}", [128, NT, D]), sb(f"x1beta{i}", [128, NT, D])
                w.xmix = sb(f"xmix{i}", [128, T])
                w.gateT = sb(f"gateT{i}", [128, T])
                w.best, w.rank = sb(f"best{i}", [128, NT]), sb(f"rank{i}", [128, NT, NP])
                w.onehot, w.onehotT = sb(f"onehot{i}", [128, NT, NP]), sb(f"onehotT{i}", [NP, T], BF16)
                w.hid, w.hid_sel = sb(f"hid{i}", [GW + NP, G3, T]), sb(f"hid_sel{i}", [GW + NP, G3, T])
                w.ffn, w.fin = sb(f"ffn{i}", [128, NT, D]), sb(f"fin{i}", [128, NT, D])
                w.s_xres, w.s_stored = sem(f"residual_x_loaded{i}"), sem(f"output_stored{i}")

        works = [WorkBuffers(i) for i in range(2)]

        def bank(name):
            return ctx.enter_context(nc.psum_tensor(name, [128, 512], F32))

        score_bank = [bank(f"score_bank{i}") for i in range(S_BUFS)]
        prob_bank = [bank(f"prob_bank{i}") for i in range(ST_BUFS)]
        out_bank = bank("out_bank")
        proj_bank = bank("proj_bank")
        post_bank = bank("post_bank")

        q_scratch = nc.dram_tensor("q_scratch", [B, QUADS, 2, TERMS, DK, PAIRS, T], BF16).ap()
        k_scratch = nc.dram_tensor("k_scratch", [B, QUADS, 2, TERMS, DK, PAIRS, T], BF16).ap()

        s_xT = [sem("even_xT_loaded"), sem("odd_xT_loaded")]
        s_wqk, s_wv, s_consts = sem("wqk_loaded"), sem("wv_loaded"), sem("consts_loaded")
        s_pool0, s_vec0, s_zero = sem("pool_setup"), sem("vector_setup"), sem("zeroed")
        s_bqk = sem("q_bias_scaled")
        s_q_mm, s_q = sem("q_product"), sem("q_ready")
        s_k_mm, s_k = sem("k_product"), sem("k_ready")
        s_v_mm, s_v = sem("v_product"), sem("v_ready")
        s_qs, s_ks = sem("q_parts_ready"), sem("k_parts_ready")
        s_qw, s_kw = sem("q_scratch_written"), sem("k_scratch_written")
        s_vb = sem("v_block_ready")
        s_sload = [sem(f"score_operands_loaded{q}") for q in range(QUADS)]
        s_tload = [sem(f"prob_operands_loaded{q}") for q in range(QUADS)]
        s_score_mm, s_score_max = sem("score_bank_filled"), sem("score_bank_reduced")
        s_nparts, s_nT_mm = sem("max_parts_ready"), sem("max_transposed_product")
        s_nT, s_shift = sem("max_rows_ready"), sem("shift_rows_loaded")
        s_prob_mm, s_exp, s_pv = sem("prob_bank_filled"), sem("probs_ready"), sem("probs_used")
        s_osb = sem("attention_out_taken")
        s_post_mm = sem("post_product_ready")
        s_post_taken = {"act": sem("post_product_taken_by_scalar"), "dve": sem("post_product_taken_by_vector")}
        s_xb = sem("residual_biased")
        s_nmean = sem("mean_ready")
        s_mv, s_var, s_x1, s_x1b = sem("moments_ready"), sem("variance_ready"), sem("x1_ready"), sem("x1_beta_ready")
        s_xmid, s_stats, s_rstd = sem("middle_tap_ready"), sem("statistics_ready"), sem("inverse_deviation_ready")
        s_gate, s_onehot = sem("gate_hidden_ready"), sem("onehot_ready")
        s_ln2, s_fin = sem("ffn_normalised"), sem("output_ready")
        s_vlink, s_plink = sem("vector_chain"), sem("pool_chain")

        CONST_LOADS = 15
        SETUP_IDENT, SETUP_MASKS, SETUP_ALL = 1, 4, 8 + NP
        SETUP_Q_ZERO, SETUP_SHIFT, SETUP_VECTOR = 1, 3, 6

        def post_count(b, name):
            return POST_ORDER.index((b, name)) + 1

        def taken_count(b, name):
            return TAKEN_ORDER[TAKEN_BY[name]].index((b, name)) + 1

        def wait_taken(engine, b, *names):
            engine.wait_ge(s_post_taken[TAKEN_BY[names[0]]], max(taken_count(b, name) for name in names))

        def moments_count(b, norm):
            return MOMENTS_ORDER.index((b, norm)) + 1

        post_banks, bank_before = {}, {}
        last_user = {}
        for stage in POST_ORDER:
            if post_step(*stage) < SCORES_END:
                i = 0
            else:
                i = min(range(1 + S_BUFS), key=lambda i: POST_ORDER.index(last_user[i]) if i in last_user else -1)
            post_banks[stage] = ([post_bank] + score_bank)[i]
            bank_before[stage] = last_user.get(i)
            last_user[i] = stage

        out_v = out.rearrange("b (n p) d -> b p n d", p=128)
        x_v = x.rearrange("b (n p) d -> b p n d", p=128)
        q_rows = q_scratch.rearrange("b q s t d p n -> b q (s t d) (p n)")
        k_rows = k_scratch.rearrange("b q s t d p n -> b q (s t d) (p n)")
        q_term = q_scratch.rearrange("b q s t d p n -> b t (q s) (d p n)")
        k_term = k_scratch.rearrange("b q s t d p n -> b t (q s) (d p n)")
        Q_PART = [0, 1, 2, 0, 1, 0]
        K_PART = [0, 0, 0, 1, 1, 2]

        def block_cols(t, q, rows, p, j):
            return t[0:rows, q, p * NJ + j, :, :].rearrange("r s w -> r (s w)")

        def normalise(engine, w, dst, src, n):
            return engine.tensor_scalar(dst[:, n, :], src[:, n, :], w.nmean[:, n:n + 1], w.rstd[:, n:n + 1], ALU.add, ALU.mult)

        def wide(t):
            return t[:, :].unsqueeze(1).broadcast_to([128, NT, D])

        def flat(t, q):
            return t[:, q, :, :].rearrange("r p n -> r (p n)")

        block = ctx.enter_context(nc.Block())

        @block.sync
        def _(sp):
            sp.dma_start(wq[:, :], Wq).then_inc(s_wqk, 16)
            sp.dma_start(xT[:, 0, :], xT_in[0]).then_inc(s_xT[0], 16)
            sp.dma_start(bqk_raw[:, :], bqk_in).then_inc(s_wqk, 16)
            sp.dma_start(wk[:, :], Wk).then_inc(s_wqk, 16)
            sp.dma_start(wv[:, :], Wv).then_inc(s_wv, 16)
            sp.dma_start(xT[:, 1, :], xT_in[1]).then_inc(s_xT[1], 16)

            def write_scratch(b):
                for part in range(3):
                    sp.wait_ge(s_qs, 3 * b + part + 1)
                    for t in range(TERMS):
                        if Q_PART[t] == part:
                            sp.dma_start(q_term[b, t], qs[:, part, :]).then_inc(s_qw, 16)
                for part in range(3):
                    sp.wait_ge(s_ks, 3 * b + part + 1)
                    for t in range(TERMS):
                        if K_PART[t] == part:
                            sp.dma_start(k_term[b, t], ks[:, part, :]).then_inc(s_kw, 16)

            def load_score_operands(u):
                b, q = divmod(u, QUADS)
                sp.wait_ge(s_qw, 16 * TERMS * (b + 1))
                if u >= QUADS:
                    sp.wait_ge(s_score_mm, STEPS * (u - QUADS + 1))
                if u < QUADS:
                    sp.wait_ge(s_vec0, SETUP_Q_ZERO)
                for s in range(2):
                    r = slice(s * ROWS, (s + 1) * ROWS)
                    sp.dma_start(q_block[r, q, :, s, :], q_rows[b, q, r].rearrange("r (c w) -> r c w", w=W)).then_inc(s_sload[q], 16)
                sp.wait_ge(s_kw, 16 * TERMS * (b + 1))
                sp.dma_start(flat(k_plain, q)[0:SHIFT, :], k_rows[b, q]).then_inc(s_sload[q], 16)

            def load_prob_operands(u):
                b, q = divmod(u, QUADS)
                if u >= QUADS:
                    sp.wait_ge(s_prob_mm, NB * (u - QUADS + 1))
                else:
                    sp.wait_ge(s_zero, 1)
                for s in range(2):
                    r = slice(s * ROWS, (s + 1) * ROWS)
                    sp.dma_start(k_block[r, q, :, s, :], k_rows[b, q, r].rearrange("r (c w) -> r c w", w=W)).then_inc(s_tload[q], 16)
                sp.dma_start(flat(q_plain, q)[0:SHIFT, :], q_rows[b, q]).then_inc(s_tload[q], 16)

            def store(b):
                w = works[b % 2]
                for n in range(0, NT, 2):
                    sp.wait_ge(s_fin, NT * b + n + 2)
                    sp.dma_start(out_v[b][:, n:n + 2], w.fin[:, n:n + 2, :]).then_inc(w.s_stored, 16)

            write_scratch(0)
            load_score_operands(0)
            load_prob_operands(0)
            load_score_operands(1)
            loads = [(bv_all[:, :], bv.partition_broadcast(128)), (wo[:, :], Wo),
                     (bo_all[:, :], bo.partition_broadcast(128)),
                     (gamma_all[:, :], gamma.partition_broadcast(128)),
                     (beta_all[:, :], beta.partition_broadcast(128)),
                     (mixc[:, :], mix),
                     (w1[:, 0:GW], W1[:, 0:GW]), (w1[:, GW:GW + DM], Wo1), (w1[:, GW + DM:], W1[:, GW:]),
                     (b1c[:, :], b1), (bg1[GW:GW + DM, :], bo1.unsqueeze(1)),
                     (w2[0:GW, :, :], W2),
                     (w2[GW:GW + NP, G3 - 1, :], b2),
                     (wg2[GW:GW + DM, :], Wo2), (bg2[:, :], bo2.partition_broadcast(128))]
            assert len(loads) == CONST_LOADS
            for dst, src in loads:
                sp.dma_start(dst, src).then_inc(s_consts, 16)
            for step in range(ALL_STEPS):
                slot, k = divmod(step, STEPS)
                if k == 0 and slot < UNITS:
                    if slot % 2 == 0 and 2 <= slot // 2 + 1 < B:
                        b = slot // 2 + 1
                        sp.wait_ge(s_v_mm, b - 1)
                        sp.dma_start(xT[:, b % 2, :], xT_in[b]).then_inc(s_xT[b % 2], 16)
                if k == SCORE_LOAD_OFF and 2 <= slot + 1 < UNITS:
                    load_score_operands(slot + 1)
                if k == PROB_LOAD_OFF and 1 <= slot < UNITS:
                    load_prob_operands(slot)
                if k == WRITE_OFF and slot < UNITS and slot % 2 == 0 and slot // 2 + 1 < B:
                    write_scratch(slot // 2 + 1)
                if step + 2 in POST_AT and POST_AT[step + 2][1] == "o0":
                    b = POST_AT[step + 2][0]
                    w = works[b % 2]
                    if b >= 2:
                        wait_taken(sp, b - 2, "wo")
                    sp.dma_start(w.xb[:, :, :], x_v[b]).then_inc(w.s_xres, 16)
                if step in STORE_AT:
                    store(STORE_AT[step])
            for i, w in enumerate(works):
                sp.wait_ge(w.s_stored, 32 * len(range(i, B, 2)))

        @block.gpsimd
        def _(pool):
            counts = {s_qs: 3}

            def signal(ins, semaphore):
                ins.then_inc(semaphore, 1)
                counts[semaphore] = counts.get(semaphore, 0) + 1
                pool.wait_ge(semaphore, counts[semaphore])

            def link(ins):
                signal(ins, s_plink)

            link(pool.memset(ident[:, :], 0.0))
            signal(pool.affine_select(out=ident[:, :], in_=ident[:, :], compare_op=ALU.not_equal, fill=1.0, base=0,
                               pattern=[[-1, 128]], channel_multiplier=1), s_pool0)

            def split(src, parts, ready, done, b):
                pool.wait_ge(ready, b + 1)
                if b >= 1:
                    pool.wait_ge(s_qw if done is s_qs else s_kw, 16 * TERMS * b)
                signal(pool.tensor_scalar(parts[:, 0, :], src[:, :], 1.0, 1.0, ALU.mult, ALU.mult), done)
                link(pool.tensor_tensor(k_rest[:, :], src[:, :], parts[:, 0, :], ALU.subtract))
                signal(pool.tensor_scalar(parts[:, 1, :], k_rest[:, :], 1.0, 1.0, ALU.mult, ALU.mult), done)
                signal(pool.tensor_tensor(parts[:, 2, :], k_rest[:, :], parts[:, 1, :], ALU.subtract), done)

            signal(pool.memset(k_block[:, :, :, :, :].rearrange("r q c s w -> r (q c s w)").bitcast(F32), 0.0), s_zero)
            split(kf, ks, s_k, s_ks, 0)
            link(pool.memset(mask_qk[0:W, :], 0.0))
            link(pool.memset(mask_kq[0:W, :], 0.0))
            link(pool.memset(spread[:, :], 1.0))
            signal(pool.affine_select(out=mask_qk[0:W, :], in_=mask_qk[0:W, :], compare_op=ALU.is_ge, fill=NEG, base=0,
                               pattern=[[-1, W]], channel_multiplier=1), s_pool0)
            signal(pool.affine_select(out=mask_kq[0:W, :], in_=mask_kq[0:W, :], compare_op=ALU.is_ge, fill=NEG, base=0,
                               pattern=[[1, W]], channel_multiplier=-1), s_pool0)
            n = GW * G3 + NP
            link(pool.affine_select(out=spread[:, :], in_=spread[:, :], compare_op=ALU.is_ge, fill=0.0, base=0,
                                    pattern=[[1, n]], channel_multiplier=-DM))
            signal(pool.affine_select(out=spread[:, :], in_=spread[:, :], compare_op=ALU.is_ge, fill=0.0, base=DM - 1,
                               pattern=[[-1, n]], channel_multiplier=DM), s_pool0)
            link(pool.memset(v_block[:, :, :, :, :].rearrange("r q j p n -> r (q j p n)"), 0.0))
            signal(pool.memset(v_block[0:W, :, :, :, 16:17], 1.0), s_pool0)
            signal(pool.memset(v_block[W:128, :, :, :, 17:18], 1.0), s_pool0)
            link(pool.memset(minus_half[:, :], -0.5))
            for p in range(NP):
                signal(pool.memset(order[:, :, p:p + 1], float(NP - p)), s_pool0)
            for w in works:
                signal(pool.memset(w.hid[GW:GW + NP, G3 - 1, :], 1.0), s_pool0)

            def build_v_block(u):
                b, q = divmod(u, QUADS)
                pool.wait_ge(s_v, b + 1)
                if u == 0:
                    pool.wait_ge(s_consts, 16 * CONST_LOADS)
                    pool.wait_ge(s_pool0, SETUP_ALL)
                if u >= QUADS:
                    pool.wait_ge(s_pv, len(GROUPS) * (u - QUADS + 1))
                for s in range(2):
                    r = slice(s * W, (s + 1) * W)
                    bias = bv_all[r, :].rearrange("r (p s d) -> r p s d", s=2, d=DK)[:, q * PAIRS:(q + 1) * PAIRS, s, :]
                    signal(pool.tensor_tensor(v_block[r, q, :, :, s * DK:(s + 1) * DK],
                                       v_nat[r, :, q * PAIRS:(q + 1) * PAIRS, :],
                                       bias.unsqueeze(1).broadcast_to([W, NJ, PAIRS, DK]), ALU.add), s_vb)

            for step in range(ALL_STEPS):
                slot, k = divmod(step, STEPS)
                if slot < UNITS and k == VBLOCK_OFF:
                    build_v_block(slot)
                if step in PROJ_AT:
                    b, name = PROJ_AT[step]
                    if name == "q":
                        split(qf, qs, s_q, s_qs, b)
                    if name == "k":
                        split(kf, ks, s_k, s_ks, b)
                if step in POST_AT and POST_AT[step][1] == "o0":
                    b = POST_AT[step][0]
                    w = works[b % 2]
                    pool.wait_ge(w.s_xres, 16 * (b // 2 + 1))
                    signal(pool.tensor_tensor(w.xb[:, :, :], w.xb[:, :, :], wide(bo_all), ALU.add), s_xb)
                if step in MOMENTS_AT:
                    b, norm = MOMENTS_AT[step]
                    w = works[b % 2]
                    pool.wait_ge(s_var, moments_count(b, norm))
                    signal(pool.tensor_tensor(w.rstd[:, :], w.varp[:, :], minus_half[:, :], ALU.pow), s_rstd)
                    if not on_vector(b, norm):
                        pool.wait_ge(s_nmean, moments_count(b, norm))
                    if norm == 0:
                        if not on_vector(b, norm):
                            for n in range(NT):
                                signal(normalise(pool, w, w.x1, w.res, n), s_x1)
                        pool.wait_ge(s_x1, NT * (b + 1))
                        signal(pool.tensor_tensor(w.x1beta[:, :, :], w.x1[:, :, :], wide(beta_all), ALU.add), s_x1b)
                    if norm == 1 and not on_vector(b, norm):
                        for n in range(NT):
                            link(normalise(pool, w, w.ffn, w.ffn, n))
                        link(pool.tensor_tensor(w.ffn[:, :, :], w.ffn[:, :, :], wide(gamma_all), ALU.mult))
                        signal(pool.tensor_tensor(w.ffn[:, :, :], w.ffn[:, :, :], w.x1beta[:, :, :], ALU.add), s_ln2)
                    if norm == 2 and not on_vector(b, norm):
                        if b >= 2:
                            pool.wait_ge(w.s_stored, 32 * (b // 2))
                        for n in range(NT):
                            signal(normalise(pool, w, w.fin, w.ffn, n), s_fin)

        @block.scalar
        def _(act):
            scale = float(DK) ** -0.5
            act.wait_ge(s_wqk, 48)
            act.activation(bqk[:, 0:1], bqk_raw[:, 0:1], ACT.Copy, scale=scale).then_inc(s_bqk, 1)

            def project(b, name):
                if name == "q":
                    act.wait_ge(s_q_mm, b + 1)
                    act.wait_ge(s_bqk, 1)
                    if b >= 1:
                        act.wait_ge(s_qs, 3 * b)
                    act.activation(qf[:, :], proj_bank[:, :], ACT.Identity, bias=bqk[:, 0:1], scale=scale).then_inc(s_q, 1)
                if name == "k":
                    act.wait_ge(s_k_mm, b + 1)
                    if b >= 1:
                        act.wait_ge(s_ks, 3 * b)
                    act.activation(kf[:, :], proj_bank[:, :], ACT.Identity, bias=bqk_raw[:, 1:2]).then_inc(s_k, 1)
                if name == "v":
                    act.wait_ge(s_v_mm, b + 1)
                    if b >= 1:
                        act.wait_ge(s_vb, 2 * QUADS * b)
                    act.activation(v_nat[:, :, :, :].rearrange("r j p d -> r (j p d)"), proj_bank[:, :], ACT.Copy).then_inc(s_v, 1)

            def load_shift_rows(u):
                q = u % QUADS
                act.wait_ge(s_nT, u + 1)
                if u >= QUADS:
                    act.wait_ge(s_prob_mm, NB * (u - QUADS + 1))
                for s in range(2):
                    act.dma_start(flat(q_plain, q)[SHIFT + 3 * s:SHIFT + 3 * s + 3, :],
                                  nmaxT[:, s * W:(s + 1) * W]).then_inc(s_shift, 16)

            for name in ("q", "k", "v"):
                project(0, name)
            for step in range(ALL_STEPS):
                slot, k = divmod(step, STEPS)
                for u, n in PROB_AT.get(step, ()):
                    total = NB * u + n
                    g, m, _ = PROB_BANKS[n]
                    group = len(GROUPS) * u + g
                    if group >= P_BUFS and m == 0:
                        act.wait_ge(s_pv, group - P_BUFS + 1)
                    act.wait_ge(s_prob_mm, total + 1)
                    act.activation(probs[:, group % P_BUFS, m, :], prob_bank[total % ST_BUFS][:, :], ACT.Exp).then_inc(s_exp, 1)
                if k == MAXT_OFF + 1 and 1 <= slot <= UNITS:
                    u = slot - 1
                    act.wait_ge(s_nT_mm, u + 1)
                    if u >= 1:
                        act.wait_ge(s_shift, 32 * u)
                    act.activation(nmaxT[:, :], proj_bank[0:3 * PAIRS * NJ, 0:W].bitcast(BF16), ACT.Copy).then_inc(s_nT, 1)
                    load_shift_rows(u)
                if k == LAG + 1 and slot >= 2 and slot - 2 < UNITS:
                    u = slot - 2
                    act.wait_ge(s_pv, len(GROUPS) * (u + 1))
                    if u >= QUADS:
                        act.wait_ge(s_post_mm, post_count(u // QUADS - 1, f"o{u % QUADS}"))
                    act.activation(o_sb[:, u % QUADS, :], out_bank[:, :], ACT.Copy).then_inc(s_osb, 1)
                if step - 1 in PROJ_AT:
                    project(*PROJ_AT[step - 1])
                if step - 1 in POST_AT:
                    b, name = POST_AT[step - 1]
                    w, product, taken = works[b % 2], post_banks[b, name], s_post_taken[TAKEN_BY[name]]
                    ready = post_count(b, name)
                    if name == "attnT":
                        act.wait_ge(s_post_mm, ready)
                        act.activation(w.attnT[:, :], product[:, :], ACT.Copy).then_inc(taken, 1)
                    if name == "x1T":
                        act.wait_ge(s_post_mm, ready)
                        act.wait_ge(s_consts, 16 * CONST_LOADS)
                        act.wait_ge(s_pool0, SETUP_ALL)
                        act.activation(w.xmix[:, :], product[:, :], ACT.Copy, scale=mixc[:, 1:2]).then_inc(s_xmid, 1)
                    if name in ("h0", "h1", "h2"):
                        g = int(name[1])
                        act.wait_ge(s_post_mm, ready)
                        if g == 0:
                            act.activation(w.gateT[GW:GW + DM, :], product[GW:GW + DM, :], ACT.Tanh,
                                           bias=bg1[GW:GW + DM, 0:1]).then_inc(s_gate, 1)
                        act.activation(w.hid[0:GW, g, :], product[0:GW, :], ACT.Identity, bias=b1c[:, g:g + 1]).then_inc(taken, 1)
                    if name == "onehotT":
                        act.wait_ge(s_post_mm, ready)
                        act.activation(w.onehotT[:, :], product[0:NP, :], ACT.Copy).then_inc(taken, 1)

        @block.vector
        def _(dve):
            count = [0]

            def link(ins):
                count[0] += 1
                ins.then_inc(s_vlink, 1)
                dve.wait_ge(s_vlink, count[0])

            dve.memset(q_block[:, :, :, :, :].rearrange("r q c s w -> r (q c s w)").bitcast(F32), 0.0).then_inc(s_vec0, 1)
            dve.wait_ge(s_q, 1)
            dve.tensor_copy(qs[:, 0, :], qf[:, :]).then_inc(s_qs, 1)
            dve.wait_ge(s_qs, 1)
            link(dve.tensor_tensor(q_rest[:, :], qf[:, :], qs[:, 0, :], ALU.subtract))
            dve.tensor_copy(qs[:, 1, :], q_rest[:, :]).then_inc(s_qs, 1)
            dve.wait_ge(s_qs, 2)
            dve.tensor_tensor(qs[:, 2, :], q_rest[:, :], qs[:, 1, :], ALU.subtract).then_inc(s_qs, 1)
            dve.wait_ge(s_pool0, SETUP_IDENT)
            dve.tensor_copy(identb[:, :], ident[:, :]).then_inc(s_vec0, 1)
            dve.wait_ge(s_zero, 1)
            link(dve.memset(k_block[SHIFT:SHIFT + 3, :, :, 0, :].bitcast(F32), ONES))
            link(dve.memset(k_block[SHIFT:SHIFT + 6, :, :, 1, :].bitcast(F32), ONES))
            dve.memset(k_block[SHIFT:SHIFT + 3, :, :, 1, :].bitcast(F32), 0.0).then_inc(s_vec0, 1)
            dve.wait_ge(s_vec0, SETUP_SHIFT)
            dve.wait_ge(s_pool0, SETUP_MASKS)
            dve.tensor_copy(mask_qk[W:128, :], mask_qk[0:W, :]).then_inc(s_vec0, 1)
            dve.tensor_copy(mask_kq[W:128, :], mask_kq[0:W, :]).then_inc(s_vec0, 1)
            dve.tensor_copy(spread[:, GW * G3:GW * G3 + NP], identb[0:NP, 0:NP]).then_inc(s_vec0, 1)

            def statistics(b, norm):
                w = works[b % 2]
                if norm == 2:
                    dve.wait_ge(s_ln2, b + 1)
                else:
                    wait_taken(dve, b, ("wo", "y")[norm])
                for n in range(NT):
                    dve.bn_stats(w.stats[:, n, :], (w.res if norm == 0 else w.ffn)[:, n, :]).then_inc(s_stats, 1)

            def moments(b, norm):
                w = works[b % 2]
                if norm == 0 and b >= 2:
                    dve.wait_ge(s_fin, NT * (b - 1))
                dve.wait_ge(s_stats, NT * moments_count(b, norm))
                for n in range(NT):
                    dve.bn_aggr(w.mv[:, n, :], w.stats[:, n, :]).then_inc(s_mv, 1)
                dve.wait_ge(s_mv, NT * moments_count(b, norm))
                dve.tensor_scalar(w.varp[:, :], w.mv[:, :, 1], EPS, 1.0, ALU.add, ALU.mult).then_inc(s_var, 1)
                dve.tensor_scalar(w.nmean[:, :], w.mv[:, :, 0], -1.0, 1.0, ALU.mult, ALU.mult).then_inc(s_nmean, 1)
                if on_vector(b, norm):
                    dve.wait_ge(s_nmean, moments_count(b, norm))
                    if norm == 0:
                        dve.wait_ge(s_rstd, moments_count(b, norm))
                        for n in range(NT):
                            normalise(dve, w, w.x1, w.res, n).then_inc(s_x1, 1)
                    if norm == 1:
                        for n in range(NT):
                            ins = dve.scalar_tensor_tensor(out=w.ffn[:, n, :], in0=w.ffn[:, n, :], scalar=w.nmean[:, n:n + 1],
                                                           in1=gamma_all[:, :], op0=ALU.add, op1=ALU.mult)
                        link(ins)
                        dve.wait_ge(s_rstd, moments_count(b, norm))
                        dve.wait_ge(s_x1b, b + 1)
                        for n in range(NT):
                            ins = dve.scalar_tensor_tensor(out=w.ffn[:, n, :], in0=w.ffn[:, n, :], scalar=w.rstd[:, n:n + 1],
                                                           in1=w.x1beta[:, n, :], op0=ALU.mult, op1=ALU.add)
                        ins.then_inc(s_ln2, 1)
                    if norm == 2:
                        dve.wait_ge(s_rstd, moments_count(b, norm))
                        dve.wait_ge(s_fin, NT * b)
                        dve.wait_ge(w.s_stored, 32 * (b // 2))
                        for n in range(NT):
                            normalise(dve, w, w.fin, w.ffn, n).then_inc(s_fin, 1)

            for step in range(ALL_STEPS):
                slot, k = divmod(step, STEPS)
                if slot < UNITS:
                    j, p, n = SCORE_BANKS[k]
                    L = (j + 1) * W
                    total = STEPS * slot + k
                    dve.wait_ge(s_score_mm, total + 1)
                    dve.tensor_reduce(nmax[:, :].rearrange("r (p j) -> r p j", j=NJ)[:, p:p + n, j],
                                      score_bank[total % S_BUFS][:, 0:n * L].rearrange("r (p l) -> r p l", l=L),
                                      AX.X, ALU.max, negate=True).then_inc(s_score_max, 1)
                    if k == STEPS - 1:
                        u = slot
                        dve.wait_ge(s_score_max, STEPS * (u + 1))
                        if u >= 1:
                            dve.wait_ge(s_nT_mm, u)
                        link(dve.tensor_copy(nmax_parts[:, 0, :], nmax[:, :]))
                        link(dve.tensor_tensor(nmax_rest[:, :], nmax[:, :], nmax_parts[:, 0, :], ALU.subtract))
                        link(dve.tensor_copy(nmax_parts[:, 1, :], nmax_rest[:, :]))
                        dve.tensor_tensor(nmax_parts[:, 2, :], nmax_rest[:, :], nmax_parts[:, 1, :], ALU.subtract).then_inc(s_nparts, 1)
                if step - 1 in POST_AT:
                    b, name = POST_AT[step - 1]
                    w, product, taken = works[b % 2], post_banks[b, name], s_post_taken[TAKEN_BY[name]]
                    ready = post_count(b, name)
                    if name in ("o0", "o1"):
                        q = int(name[1])
                        dve.wait_ge(s_post_mm, ready)
                        if taken_count(b, name) > 1:
                            dve.wait_ge(taken, taken_count(b, name) - 1)
                        o = product[:, :].rearrange("r (n p c) -> r n p c", p=PAIRS, c=32)
                        link(dve.reciprocal(w.o_rden[:, :, :, :], o[:, :, :, 16:18]))
                        heads = w.attn[:, :, q * D // 2:(q + 1) * D // 2].rearrange("r n (p s d) -> r n p s d", s=2, d=DK)
                        for s in range(2):
                            ins = dve.tensor_tensor(heads[:, :, :, s, :], o[:, :, :, s * DK:(s + 1) * DK],
                                                    w.o_rden[:, :, :, s:s + 1].broadcast_to([128, NT, PAIRS, DK]), ALU.mult)
                        ins.then_inc(taken, 1)
                    if name == "wo":
                        dve.wait_ge(s_post_mm, ready)
                        dve.wait_ge(s_xb, b + 1)
                        if b >= 2:
                            dve.wait_ge(s_x1, NT * (b - 1))
                        dve.tensor_tensor(w.res[:, :, :].rearrange("r n d -> r (n d)"), product[:, :],
                                          w.xb[:, :, :].rearrange("r n d -> r (n d)"), ALU.add).then_inc(taken, 1)
                    if name == "gate":
                        dve.wait_ge(s_post_mm, ready)
                        sc = product[:, 0:NT * NP].rearrange("r (n p) -> r n p", p=NP)
                        dve.tensor_tensor(w.rank[:, :, :], sc, bg2[:, :].unsqueeze(1).broadcast_to([128, NT, NP]),
                                          ALU.add).then_inc(taken, 1)
                        wait_taken(dve, b, name)
                        link(dve.tensor_reduce(w.best[:, :], w.rank[:, :, :], AX.X, ALU.max))
                        link(dve.tensor_tensor(w.rank[:, :, :], w.rank[:, :, :], w.best[:, :].unsqueeze(2).broadcast_to([128, NT, NP]),
                                               ALU.is_equal))
                        link(dve.tensor_tensor(w.rank[:, :, :], w.rank[:, :, :], order[:, :, :], ALU.mult))
                        link(dve.tensor_reduce(w.best[:, :], w.rank[:, :, :], AX.X, ALU.max))
                        dve.tensor_tensor(w.onehot[:, :, :], w.rank[:, :, :], w.best[:, :].unsqueeze(2).broadcast_to([128, NT, NP]),
                                          ALU.is_equal).then_inc(s_onehot, 1)
                    if name in ("m0", "m1", "m2"):
                        g = int(name[1])
                        n = GW + (NP if g == G3 - 1 else 0)
                        dve.wait_ge(s_post_mm, ready)
                        wait_taken(dve, b, f"h{g}")
                        dve.tensor_tensor(w.hid_sel[0:n, g, :], product[0:n, :], w.hid[0:n, g, :], ALU.mult).then_inc(taken, 1)
                    if name == "y":
                        dve.wait_ge(s_post_mm, ready)
                        if b >= 2:
                            dve.wait_ge(s_fin, NT * (b - 1))
                        dve.tensor_tensor(w.ffn[:, :, :].rearrange("r n d -> r (n d)"), product[:, :],
                                          w.x1[:, :, :].rearrange("r n d -> r (n d)"), ALU.add).then_inc(taken, 1)
                if step - 2 in POST_AT and POST_AT[step - 2][1] == "x1T":
                    b, name = POST_AT[step - 2]
                    w, product = works[b % 2], post_banks[b, name]
                    dve.wait_ge(s_xmid, b + 1)
                    link(dve.scalar_tensor_tensor(out=w.xmix[:, 1:T], in0=product[:, 0:T - 1], scalar=mixc[:, 0:1],
                                                  in1=w.xmix[:, 1:T], op0=ALU.mult, op1=ALU.add))
                    dve.scalar_tensor_tensor(out=w.xmix[:, 0:T - 1], in0=product[:, 1:T], scalar=mixc[:, 2:3],
                                             in1=w.xmix[:, 0:T - 1], op0=ALU.mult, op1=ALU.add).then_inc(s_post_taken["dve"], 1)
                if step in MOMENTS_AT:
                    statistics(*MOMENTS_AT[step])
                if step - 1 in MOMENTS_AT:
                    moments(*MOMENTS_AT[step - 1])

        @block.tensor
        def _(pe):
            def project(b, name):
                if name == "q":
                    pe.wait_ge(s_xT[b % 2], 16 * (b // 2 + 1))
                    if b == 0:
                        pe.wait_ge(s_wqk, 48)
                    else:
                        pe.wait_ge(s_v, b)
                        if b >= 2:
                            pe.wait_ge(s_nT, 2 * b - 2)
                    pe.matmul(proj_bank[:, :], wq[:, :], xT[:, b % 2, :], start=True, stop=True).then_inc(s_q_mm, 1)
                if name == "k":
                    pe.wait_ge(s_q, b + 1)
                    pe.matmul(proj_bank[:, :], wk[:, :], xT[:, b % 2, :], start=True, stop=True).then_inc(s_k_mm, 1)
                if name == "v":
                    pe.wait_ge(s_k, b + 1)
                    if b == 0:
                        pe.wait_ge(s_wv, 16)
                    else:
                        pe.wait_ge(s_nT, 2 * b - 1)
                    for j in range(NJ):
                        for s in range(2):
                            mm = pe.matmul(proj_bank[s * W:(s + 1) * W, j * W:(j + 1) * W], xT[:, b % 2, j * W:(j + 1) * W],
                                           wv[:, :].rearrange("c (p s d) -> c s p d", s=2, d=DK)[:, s],
                                           start=True, stop=True)
                    mm.then_inc(s_v_mm, 1)

            for name in ("q", "k", "v"):
                project(0, name)
            pe.wait_ge(s_vec0, SETUP_VECTOR)
            pending = []

            def weigh(u, g):
                group = len(GROUPS) * u + g
                q = u % QUADS
                pe.wait_ge(s_exp, NB * u + sum(len(x) for x in GROUPS[:g + 1]))
                if g == 0:
                    pe.wait_ge(s_vb, 2 * (u + 1))
                    if u >= 1:
                        pe.wait_ge(s_osb, u)
                parts = {}
                for m, bank_parts in enumerate(GROUPS[g]):
                    for j, p, col in bank_parts:
                        parts.setdefault(j, []).append((p, m, col))
                for j, items in parts.items():
                    for p, m, col in items:
                        L = T - j * W
                        mm = pe.matmul(out_bank[32 * p:32 * p + 32, j * W:T], v_block[:, q, j, p, :],
                                       probs[:, group % P_BUFS, m, col:col + L],
                                       start=(g == 0), stop=(g == len(GROUPS) - 1), skip_group_check=True)
                mm.then_inc(s_pv, 1)

            for step in range(ALL_STEPS):
                slot, k = divmod(step, STEPS)
                if slot < UNITS:
                    u, q = slot, slot % QUADS
                    total = STEPS * u + k
                    if k == 0:
                        pe.wait_ge(s_sload[q], 48 * (u // QUADS + 1))
                    if total >= S_BUFS:
                        pe.wait_ge(s_score_max, total - S_BUFS + 1)
                    j, p0, n = SCORE_BANKS[k]
                    L = (j + 1) * W
                    dst = score_bank[total % S_BUFS]
                    for i in range(n):
                        pe.matmul(dst[:, i * L:(i + 1) * L], block_cols(q_block, q, SHIFT, p0 + i, j),
                                  k_plain[0:SHIFT, q, p0 + i, 0:L], start=True, stop=False)
                        mm = pe.matmul(dst[:, (i + 1) * L - W:(i + 1) * L], identb[:, :], mask_qk[:, :], start=False, stop=True)
                    mm.then_inc(s_score_mm, 1)
                for u, n in PROB_AT.get(step, ()):
                    q = u % QUADS
                    total = NB * u + n
                    if n == 0:
                        pe.wait_ge(s_tload[q], 48 * (u // QUADS + 1))
                        pe.wait_ge(s_shift, 32 * (u + 1))
                    if total >= ST_BUFS:
                        pe.wait_ge(s_exp, total - ST_BUFS + 1)
                    dst = prob_bank[total % ST_BUFS]
                    for j, p, col in PROB_BANKS[n][2]:
                        L = T - j * W
                        pe.matmul(dst[:, col:col + L], block_cols(k_block, q, KST, p, j),
                                  q_plain[0:KST, q, p, j * W:T], start=True, stop=False)
                        mm = pe.matmul(dst[:, col:col + W], identb[:, :], mask_kq[:, :], start=False, stop=True)
                    mm.then_inc(s_prob_mm, 1)
                    g, m, _ = PROB_BANKS[n]
                    if m == len(GROUPS[g]) - 1:
                        pending.append((u, g, total))
                    while pending and (pending[0][2] <= total - 2):
                        weigh(*pending.pop(0)[:2])
                if k == LAG and slot >= 2 and slot - 2 < UNITS:
                    while pending and pending[0][0] <= slot - 2:
                        weigh(*pending.pop(0)[:2])
                if k == MAXT_OFF and 1 <= slot <= UNITS:
                    u = slot - 1
                    pe.wait_ge(s_nparts, u + 1)
                    if u % 2 == 0 and u // 2 + 1 < B:
                        pe.wait_ge(s_k, u // 2 + 2)
                    if u % 2 == 1 and (u + 1) // 2 < B:
                        pe.wait_ge(s_v, (u + 1) // 2 + 1)
                    if u >= 1:
                        pe.wait_ge(s_nT, u)
                    pe.transpose(proj_bank[0:3 * PAIRS * NJ, 0:W].bitcast(BF16), nmax_parts[:, :, :].rearrange("r t c -> r (t c)"),
                                 identb[:, :]).then_inc(s_nT_mm, 1)
                if step in PROJ_AT:
                    project(*PROJ_AT[step])
                if step in POST_AT:
                    b, name = POST_AT[step]
                    w, product = works[b % 2], post_banks[b, name]
                    if bank_before[b, name]:
                        wait_taken(pe, *bank_before[b, name])
                    elif post_step(b, name) >= SCORES_END:
                        pe.wait_ge(s_score_max, STEPS * UNITS)
                    if name in ("o0", "o1"):
                        q = int(name[1])
                        pe.wait_ge(s_osb, QUADS * b + q + 1)
                        for n in range(NT):
                            mm = pe.transpose(product[:, n * 128:(n + 1) * 128], o_sb[:, q, n * 128:(n + 1) * 128], ident[:, :])
                    if name == "attnT":
                        wait_taken(pe, b, "o0", "o1")
                        for n in range(NT):
                            mm = pe.transpose(product[:, n * 128:(n + 1) * 128], w.attn[:, n, :], ident[:, :])
                    if name == "wo":
                        wait_taken(pe, b, "attnT")
                        pe.wait_ge(s_consts, 16 * CONST_LOADS)
                        for n in range(NT):
                            mm = pe.matmul(product[:, n * 128:(n + 1) * 128], w.attnT[:, n * 128:(n + 1) * 128], wo[:, :],
                                           start=True, stop=True)
                    if name == "x1T":
                        for n in range(NT):
                            pe.wait_ge(s_x1, NT * b + n + 1)
                            mm = pe.transpose(product[:, n * 128:(n + 1) * 128], w.x1[:, n, :], ident[:, :])
                    if name == "gate":
                        pe.wait_ge(s_gate, b + 1)
                        for n in range(NT):
                            mm = pe.matmul(product[:, n * NP:(n + 1) * NP], w.gateT[GW:GW + DM, n * 128:(n + 1) * 128],
                                           wg2[GW:GW + DM, :], start=True, stop=True)
                    if name in ("h0", "h1", "h2"):
                        g = int(name[1])
                        wait_taken(pe, b, "x1T")
                        c, n = (0, GW + DM) if g == 0 else (g * GW + DM, GW)
                        mm = pe.matmul(product[0:n, :], w1[:, c:c + n], w.xmix[:, :], start=True, stop=True)
                    if name == "onehotT":
                        pe.wait_ge(s_onehot, b + 1)
                        for n in range(NT):
                            mm = pe.transpose(product[0:NP, n * 128:(n + 1) * 128], w.onehot[:, n, :], ident[:, :])
                    if name in ("m0", "m1", "m2"):
                        wait_taken(pe, b, "onehotT")
                        g = int(name[1])
                        n = GW + (NP if g == G3 - 1 else 0)
                        mm = pe.matmul(product[0:n, :], spread[:, g * GW:g * GW + n], w.onehotT[:, :], start=True, stop=True)
                    if name == "y":
                        for g in range(G3):
                            wait_taken(pe, b, f"m{g}")
                            r = GW + (NP if g == G3 - 1 else 0)
                            for n in range(NT):
                                mm = pe.matmul(product[:, n * 128:(n + 1) * 128], w.hid_sel[0:r, g, n * 128:(n + 1) * 128],
                                               w2[0:r, g, :], start=(g == 0 and n == 0), stop=(g == G3 - 1), skip_group_check=True)
                    mm.then_inc(s_post_mm, 1)


_INS = ["x", "xT", "Wq", "bqk", "Wk", "Wv", "bv", "Wo", "bo", "mix", "W1", "b1", "W2", "b2", "Wo1", "bo1", "Wo2", "bo2",
        "gamma", "beta"]
_OUTS = [((B, T, D), "float32")]


def kernel(**inputs):
    import numpy as _np
    import concourse.bacc as _bacc
    from concourse import mybir as _mybir
    from concourse.bass_utils import run_bass_kernel_spmd as _run

    given = {n.split("_", 2)[2]: _np.asarray(a) for n, a in inputs.items() if n.startswith("L0_attn_")}
    given |= {("g" if n in ("L0_ffn_Wo1", "L0_ffn_bo1", "L0_ffn_Wo2", "L0_ffn_bo2") else "") + n.split("_", 2)[2]: _np.asarray(a)
              for n, a in inputs.items() if n.startswith("L0_ffn_")}

    def by_quad(a):
        return a.reshape(-1, QUADS, PAIRS, 2, DK).transpose(0, 1, 3, 4, 2).reshape(-1, D)

    laid = {
        "x": given["x"], "xT": given["x"].transpose(0, 2, 1),
        "Wq": by_quad(given["Wq"]), "Wk": by_quad(given["Wk"]),
        "bqk": _np.stack([by_quad(given["bq"])[0], by_quad(given["bk"])[0]], axis=1),
        "Wv": given["Wv"], "bv": given["bv"], "Wo": given["Wo"], "bo": given["bo"],
        "mix": given["mix_kernel"].T, "W1": given["W1"].transpose(1, 0, 2).reshape(D, NP * DM),
        "b1": given["b1"].reshape(G3, GW).T, "W2": given["W2"].reshape(G3, GW, D).transpose(1, 0, 2), "b2": given["b2"],
        "Wo1": given["gWo1"], "bo1": given["gbo1"], "Wo2": given["gWo2"], "bo2": given["gbo2"],
        "gamma": given["gamma"], "beta": given["beta"],
    }
    nc = _bacc.Bacc("TRN2", target_bir_lowering=False, num_devices=1)
    arrays, args = {}, []
    for name in _INS:
        a = _np.ascontiguousarray(laid[name])
        arrays[f"in_{name}_dram"] = a
        args.append(nc.dram_tensor(f"in_{name}_dram", a.shape, _mybir.dt.from_np(a.dtype), kind="ExternalInput").ap())
    for i, (shape, dtype) in enumerate(_OUTS):
        dt = _mybir.dt.from_np(_np.dtype(dtype))
        args.append(nc.dram_tensor(f"out_{i}_dram", shape, dt, kind="ExternalOutput").ap())
    postln_block(nc, *args)
    r = _run(nc, [arrays], core_ids=[0])
    return r.results[0]["out_0_dram"]
```
